# Optimizing a Trainium2 kernel written in Bass

```python
import numpy as np
import jax
import jax.numpy as jnp

def _softmax(x, axis=-1):
    return jax.nn.softmax(x, axis=axis)

def _gelu(x):
    return jax.nn.gelu(x, approximate=True)

def _silu(x):
    return jax.nn.silu(x)

def _sigmoid(x):
    return jax.nn.sigmoid(x)

def _layernorm(x, axis=-1, eps=1e-05):
    m = jnp.mean(x, axis=axis, keepdims=True)
    v = jnp.var(x, axis=axis, keepdims=True)
    return (x - m) / jnp.sqrt(v + eps)

def _scatter_add(tgt, idx, src, axis=0):
    return tgt.at[idx].add(src)

def _segment_sum(src, seg, n):
    return jax.ops.segment_sum(src, seg, n)
kernel_name = 'mk_prb_d1_jaxref_r8_32aa2c'

def setup_inputs(seed: int=0):
    np.random.seed(seed)
    _w = jnp.asarray

    def _L0_attn_setup():
        import jax, jax.numpy as jnp
        import numpy as np
        D_MODEL = 128
        NUM_HEADS = 16
        B, S = (1, 512)
        key = jax.random.key(seed)
        kx, kq, kk, kv, ko = jax.random.split(key, 5)
        std = (1.0 / D_MODEL) ** 0.5

        def trunc(k):
            return std * jax.random.truncated_normal(k, -3.0, 3.0, (D_MODEL, D_MODEL), dtype=jnp.float32)
        return {'x': jax.random.normal(kx, (B, S, D_MODEL), dtype=jnp.float32), 'W_Q': trunc(kq), 'W_K': trunc(kk), 'W_V': trunc(kv), 'W_O': trunc(ko)}
    _L0_attn_in = _L0_attn_setup()

    def _L0_ffn_setup():
        import jax, jax.numpy as jnp
        import numpy as np
        E = 8
        TOPK = 2

        def _moe_forward(x, Wg, W1, W2, W3):
            B, S, D = x.shape
            xt = x.reshape(-1, D)
            T = xt.shape[0]
            logits = xt @ Wg.T
            scores = jax.nn.softmax(logits, axis=-1)
            w, idx = jax.lax.top_k(scores, TOPK)
            w = w / (w.sum(axis=-1, keepdims=True) + 1e-20)
            cw = jnp.zeros((T, E), xt.dtype).at[jnp.arange(T)[:, None], idx].add(w)
            h = jax.nn.silu(jnp.einsum('td,ehd->teh', xt, W1)) * jnp.einsum('td,ehd->teh', xt, W3)
            out = jnp.einsum('teh,edh->ted', h, W2)
            y = jnp.einsum('te,ted->td', cw, out)
            return y.reshape(B, S, D)
        key = jax.random.key(seed)
        k0, k1, k2, k3, k4 = jax.random.split(key, 5)
        B, S, D, H = (1, 256, 128, 352)
        scale = 0.02
        x = jax.random.normal(k0, (B, S, D), jnp.float32)
        Wg = jax.random.normal(k1, (E, D), jnp.float32) * scale
        W1 = jax.random.normal(k2, (E, H, D), jnp.float32) * scale
        W2 = jax.random.normal(k3, (E, D, H), jnp.float32) * scale
        W3 = jax.random.normal(k4, (E, H, D), jnp.float32) * scale
        return {'x': x, 'Wg': Wg, 'W1': W1, 'W2': W2, 'W3': W3}
    _L0_ffn_in = _L0_ffn_setup()
    _d = {'L0_attn_x': _L0_attn_in['x'], 'L0_attn_W_Q': _L0_attn_in['W_Q'], 'L0_attn_W_K': _L0_attn_in['W_K'], 'L0_attn_W_V': _L0_attn_in['W_V'], 'L0_attn_W_O': _L0_attn_in['W_O'], 'L0_ffn_Wg': _L0_ffn_in['Wg'], 'L0_ffn_W1': _L0_ffn_in['W1'], 'L0_ffn_W2': _L0_ffn_in['W2'], 'L0_ffn_W3': _L0_ffn_in['W3']}
    _x0 = _d['L0_attn_x']
    _d['L0_attn_x'] = jax.random.normal(jax.random.fold_in(jax.random.key(seed), 1), (2, 1024, 128), dtype=_x0.dtype)
    del _x0
    return _d

def reference(L0_attn_x, L0_attn_W_Q, L0_attn_W_K, L0_attn_W_V, L0_attn_W_O, L0_ffn_Wg, L0_ffn_W1, L0_ffn_W2, L0_ffn_W3):

    def _L0_attn_ref(x, W_Q, W_K, W_V, W_O):
        import jax, jax.numpy as jnp
        import numpy as np
        D_MODEL = 128
        NUM_HEADS = 16
        B, S = (1, 512)
        Bx, Sx, Dm = x.shape
        H = NUM_HEADS
        d_attn = Dm // H
        Q = x @ W_Q.T
        K = x @ W_K.T
        V = x @ W_V.T
        Q = Q.reshape(Bx, Sx, H, d_attn).transpose(0, 2, 1, 3)
        K = K.reshape(Bx, Sx, H, d_attn).transpose(0, 2, 1, 3)
        V = V.reshape(Bx, Sx, H, d_attn).transpose(0, 2, 1, 3)
        scale = 1.0 / jnp.sqrt(jnp.asarray(d_attn, dtype=x.dtype))
        attn = jnp.einsum('bhqd,bhkd->bhqk', Q, K) * scale
        causal = jnp.tril(jnp.ones((Sx, Sx), dtype=bool))
        attn = jnp.where(causal, attn, jnp.asarray(-jnp.inf, dtype=attn.dtype))
        probs = jax.nn.softmax(attn, axis=-1)
        y = jnp.einsum('bhqk,bhkd->bhqd', probs, V)
        y = y.transpose(0, 2, 1, 3).reshape(Bx, Sx, Dm)
        return y @ W_O.T

    def _L0_ffn_ref(x, Wg, W1, W2, W3):
        import jax, jax.numpy as jnp
        import numpy as np
        E = 8
        TOPK = 2

        def _moe_forward(x, Wg, W1, W2, W3):
            B, S, D = x.shape
            xt = x.reshape(-1, D)
            T = xt.shape[0]
            logits = xt @ Wg.T
            scores = jax.nn.softmax(logits, axis=-1)
            w, idx = jax.lax.top_k(scores, TOPK)
            w = w / (w.sum(axis=-1, keepdims=True) + 1e-20)
            cw = jnp.zeros((T, E), xt.dtype).at[jnp.arange(T)[:, None], idx].add(w)
            h = jax.nn.silu(jnp.einsum('td,ehd->teh', xt, W1)) * jnp.einsum('td,ehd->teh', xt, W3)
            out = jnp.einsum('teh,edh->ted', h, W2)
            y = jnp.einsum('te,ted->td', cw, out)
            return y.reshape(B, S, D)
        return _moe_forward(x, Wg, W1, W2, W3)
    x = L0_attn_x
    xn = _layernorm(x, axis=-1)
    x = x + _L0_attn_ref(xn, L0_attn_W_Q, L0_attn_W_K, L0_attn_W_V, L0_attn_W_O) + _L0_ffn_ref(xn, L0_ffn_Wg, L0_ffn_W1, L0_ffn_W2, L0_ffn_W3)
    return x

_drawn_inputs = setup_inputs


def setup_inputs(seed=0):
    import zlib

    import numpy as np

    out = dict(_drawn_inputs(seed))
    spreads = {}
    factors = {'L0_ffn_Wg': 8.0, 'L0_ffn_W1': 8.0, 'L0_ffn_W2': 8.0, 'L0_ffn_W3': 8.0}
    for name, (base, spread) in spreads.items():
        noise = np.random.default_rng([zlib.crc32(name.encode()), seed]).standard_normal(out[name].shape)
        drawn = base * np.exp(spread * noise) if base else spread * noise
        out[name] = jnp.asarray(drawn.astype(out[name].dtype))
    for name, factor in factors.items():
        out[name] = (out[name] * factor).astype(out[name].dtype)
    return out
```

```python
from contextlib import ExitStack

import concourse.bass as bass
from concourse import mybir

ALU = mybir.AluOpType
ACT = mybir.ActivationFunctionType
AX_X = mybir.AxisListType.X
F32 = mybir.dt.float32
BF16 = mybir.dt.bfloat16
U32 = mybir.dt.uint32

P = 128
NEG = -3.0e38


def layer_kernel(nc, x_in, wqkv_in, wo_in, wg_in, w1_in, w3_in, w2_in, out):
    NB, S, D = x_in.shape
    NH = 16
    HD = D // NH
    E = wg_in.shape[1]
    FH = w1_in.shape[1] // E
    FC = -(-FH // P)
    TAIL = FH - (FC - 1) * P
    NT = NB * S // P
    TB = S // P
    G = 4
    NG = NH // G
    ITS = NB * NG
    CH = 512
    SCALE = float(HD) ** -0.5
    TERMS = 6
    KR = TERMS * HD
    Q_PART = [0, 0, 1, 1, 0, 2]
    K_PART = [0, 1, 0, 1, 2, 0]

    RING = 3
    PSLOTS = 4
    LAG = 2
    A_UNITS = [(i, j, c) for i in range(TB) for j in range(G) for c in range(i * P // CH + 1)]
    NA = len(A_UNITS)
    B_STEPS = [(c, k) for c in range(S // CH) for k in range((c + 1) * CH // P)]
    NS = len(B_STEPS)
    NBU = NS * G
    DIAG = TB
    O_COPY, O_TURN = G + 1, G + 3

    def a_cols(u):
        i, j, c = A_UNITS[u]
        return min((i + 1) * P - c * CH, CH)

    def b_first(n):
        c, k = B_STEPS[n]
        return max(k * P - c * CH, 0)

    total = sum(a_cols(u) + 80 for u in range(NA))
    a_slots, done = [[] for _ in range(NS)], 0
    for u in range(NA):
        a_slots[min(done * NS // total, NS - 1)].append(u)
        done += a_cols(u) + 80

    PAIRS = NB * S * 2
    TILES = (PAIRS + E * (P - 1)) // P
    FIRST = TILES - 6 * (ITS - 2)
    FC = -(-FH // P)
    HP = FC * P
    TAIL = FH - (FC - 1) * P
    WALL = 6 * HP

    def first_tile(s):
        if isinstance(s, int) and s == 1:
            return 0, FIRST
        return FIRST + (s - 2) * 6, 6

    with ExitStack() as ctx:
        def sb(name, shape, dt):
            return ctx.enter_context(nc.sbuf_tensor(name, shape, dt))

        def sem(name):
            return ctx.enter_context(nc.semaphore(name))

        q_dram = nc.dram_tensor("q_parts", [NB * NH, KR, S], BF16).ap()
        k_dram = nc.dram_tensor("k_parts", [NB * NH, KR, S], BF16).ap()
        xs_dram = nc.dram_tensor("x_sorted", [TILES * P, 2 * D], BF16).ap()
        y_dram = nc.dram_tensor("y_sorted", [TILES * P, D], F32).ap()

        bank = [ctx.enter_context(nc.psum_tensor(f"bank{i}", [P, CH], F32)) for i in range(8)]
        ps_a, ps_b, ps_o, ps_m = bank[0:3], bank[3:6], bank[6], bank[7]
        ps_m16 = ps_m[:, :].bitcast(BF16)
        ps_h = [(ps_a[0], ps_a[1]), (ps_b[0], ps_b[1])]
        ps_x, ps_y = ps_a[2][:, :].bitcast(BF16), ps_b[2]

        x = sb("x", [P, NT, D], F32)
        xn = sb("xn", [P, NT, D], F32)
        xhl = sb("xhl", [P, NT, 2, D], BF16)
        stats = sb("stats", [P, NT, 6], F32)
        mv = sb("mv", [P, NT, 2], F32)
        veps = sb("veps", [P, NT], F32)
        sdev = sb("sdev", [P, NT], F32)
        rstd = sb("rstd", [P, NT], F32)
        identf = sb("identf", [P, P], F32)
        identb = sb("identb", [P, P], BF16)
        before = sb("before", [P, P], BF16)
        onesb = sb("onesb", [P, P], BF16)
        causal = sb("causal", [P, CH], F32)
        iota_e = sb("iota_e", [P, E], F32)
        iota_t = sb("iota_t", [P, TILES], F32)
        iota_s = sb("iota_s", [P, NT], F32)
        lower = sb("lower", [P, E, E], F32)
        zrow = sb("zrow", [P, 2 * D], BF16)
        wqkv = sb("wqkv", [P, 3 * D], F32)
        wo = sb("wo", [P, D], F32)
        wg = sb("wg", [P, E], F32)
        rest = sb("rest", [P, 2, CH], F32)
        vall = sb("vall", [P, ITS, TB, G * HD], F32)
        vw = sb("vw", [P, 2, TB, G, 32], F32)
        qa = sb("qa", [P, 2, 2, S], BF16)
        ka = sb("ka", [P, 2, G, S], BF16)
        qb = sb("qb", [P, 2, 2, S], BF16)
        kb = sb("kb", [P, 2, G, S], BF16)
        junk = sb("junk", [P, RING, CH], BF16)
        mpart = sb("mpart", [P, 2, TB, G, 2], F32)
        nmax = sb("nmax", [P, TB, G], F32)
        nmr = sb("nmr", [P, 2, TB, G], F32)
        mt = sb("mt", [P, TB, G, 3], BF16)
        mrow = sb("mrow", [3 * G, S], BF16)
        prob = sb("prob", [P, PSLOTS, G, CH], F32)
        flat = prob[:, :, :, :].rearrange("p a b c -> p (a b c)").bitcast(BF16)
        part = [[flat[:, (3 * w + i) * NB * S:(3 * w + i + 1) * NB * S] for i in range(3)] for w in range(2)]
        osb = sb("osb", [P, CH], F32)
        rden = sb("rden", [P, 4, G], F32)
        attn = sb("attn", [P, NB, TB, NG, G * HD], F32)
        xnT = attn[:, :, :, :, :].rearrange("p b t g d -> p (b t g d)")
        lg = sb("lg", [P, NT, E], F32)
        sc = sb("sc", [P, NT, E], F32)
        r1 = sb("r1", [P, NT], F32)
        r2 = sb("r2", [P, NT], F32)
        top = sb("top", [P, NT, 8], F32)
        topi = sb("topi", [P, NT, 8], U32)
        topf = sb("topf", [P, NT, 8], F32)
        gate = sb("gate", [P, 2, NT], F32)
        hot = sb("hot", [P, 2, NT, E], F32)
        both = sb("both", [P, NT, E], BF16)
        big = sb("big", [P, TILES, E], F32)
        ntile = sb("ntile", [P, E], F32)
        start = sb("start", [P, E], F32)
        posf = sb("posf", [P, 2, NT], F32)
        pos = sb("pos", [P, 2, NT], U32)
        tile_f = sb("tile_f", [P, TILES], F32)
        tile_e = sb("tile_e", [P, TILES], U32)
        wst = sb("wst", [P, 2, HP], F32)
        wall = sb("wall", [P, E, WALL], BF16)
        wbuf = sb("wbuf", [P, 2, WALL], BF16)
        ysb = sb("ysb", [P, 2, D], F32)
        xn_flat = xn[:, :, :].rearrange("p t d -> p (t d)")
        th, ha, hf = [xn_flat[:, i * HP:(i + 1) * HP] for i in range(3)]
        xn16 = xn_flat[:, 3 * HP:].bitcast(BF16)
        hh, hl = xn16[:, 0:HP], xn16[:, HP:2 * HP]
        xs, xsT = [xn16[:, 2 * HP + i * 4 * D:2 * HP + (i + 1) * 4 * D].rearrange("p (q d) -> p q d", q=2)
                   for i in range(2)]
        yg = wall[:, :, :].rearrange("p e w -> p (e w)").bitcast(F32)[:, 0:2 * NT * D].rearrange(
            "p (k t d) -> p k t d", k=2, t=NT)

        x_in_sem = [sem(f"x_in{b}") for b in range(NB)]
        wqkv_in_sem = sem("wqkv_in")
        w_in = sem("w_in")
        pool_const = sem("pool_const")
        pool_passed = sem("pool_passed")
        dve_passed = sem("dve_passed")
        op_zero = sem("op_zero")
        kb_one = sem("kb_one")
        pad_zero = sem("pad_zero")
        dve = sem("dve_chain")
        veps_ready = sem("veps_ready")
        sdev_ready = sem("sdev_ready")
        xn_ready = sem("xn_ready")
        xhi_ready = sem("xhi_ready")
        xlo_ready = sem("xlo_ready")
        xT_done = sem("xT_done")
        xnT_ready = sem("xnT_ready")
        qk_proj = sem("qk_proj")
        hi_ready = sem("hi_ready")
        rest_ready = sem("rest_ready")
        mid_ready = sem("mid_ready")
        lo_ready = sem("lo_ready")
        parts_out = sem("parts_out")
        v_proj = sem("v_proj")
        v_ready = sem("v_ready")
        logits_done = sem("logits_done")
        ex_in = sem("ex_in")
        ex_ready = sem("ex_ready")
        both_ready = sem("both_ready")
        rank_done = sem("rank_done")
        rank_read = sem("rank_read")
        pos_ready = sem("pos_ready")
        tile_e_ready = sem("tile_e_ready")
        xs_zero = sem("xs_zero")
        scattered = sem("scattered")
        a_loaded = [sem(f"a_loaded{i}") for i in range(2)]
        b_loaded = [sem(f"b_loaded{i}") for i in range(2)]
        m_loaded = sem("m_loaded")
        a_scores = sem("a_scores")
        a_used = sem("a_used")
        max_chain = sem("max_chain")
        mt_ready = sem("mt_ready")
        mT_done = sem("mT_done")
        mrow_ready = sem("mrow_ready")
        b_scores = sem("b_scores")
        exp_done = sem("exp_done")
        masked = sem("masked")
        vw_ready = sem("vw_ready")
        pv_done = sem("pv_done")
        osb_ready = sem("osb_ready")
        oT_done = sem("oT_done")
        rden_ready = sem("rden_ready")
        attn_ready = sem("attn_ready")
        yT_done = sem("yT_done")
        yT_ready = sem("yT_ready")
        y_done = sem("y_done")
        y_added = sem("y_added")
        w_stage = [sem(f"w_stage{i}") for i in range(2)]
        w_hi = sem("w_hi")
        w_lo = sem("w_lo")
        w_tail = sem("w_tail")
        w_here = [sem(f"w_here{i}") for i in range(2)]
        x_here = [sem(f"x_here{i}") for i in range(2)]
        xsT_done = sem("xsT_done")
        xsT_ready = sem("xsT_ready")
        h_done = sem("h_done")
        th_ready = sem("th_ready")
        ha_ready = sem("ha_ready")
        hf_ready = sem("hf_ready")
        hh_ready = sem("hh_ready")
        hl_ready = sem("hl_ready")
        ey_done = sem("ey_done")
        ey_ready = sem("ey_ready")
        ey_out = [sem(f"ey_out{i}") for i in range(2)]
        gathered = [sem(f"gathered{c}") for c in range(NT // 4)]
        combined = sem("combined")
        out_done = sem("out_done")

        nc.disable_value_cache = True
        block = ctx.enter_context(nc.Block())

        W_PIECES = [(k, e) for e in range(E) for k in range(3)]
        NW = len(W_PIECES)

        def w_areas(k):
            if k < 2:
                return [(slice(0, P), slice(0, FH))]
            return [(slice(0, P), slice(0, (FC - 1) * P)), (slice(0, TAIL), slice((FC - 1) * P, HP))]

        def w_part(buf, k, i, cols):
            return buf[:, (2 * k + i) * HP + cols.start:(2 * k + i) * HP + cols.stop]

        def known(s, *values):
            return isinstance(s, int) and s in values

        def loads(s, par):
            return 16 * (s // 2 + 1) if isinstance(s, int) else 8 * (s - par) + 16

        def parity(s, k):
            return k % 2 if known(s, 1) else (k + FIRST) % 2

        def tile_loads(s, k):
            T, _ = first_tile(s)
            if isinstance(s, int):
                return 16 * ((T + k) // 2 + 1)
            return 8 * (T + k - parity(s, k)) + 16

        @block.sync
        def _(sp):
            for b in range(NB):
                sp.dma_start(x[:, b * TB:(b + 1) * TB, :],
                             x_in[b].rearrange("(t p) d -> p t d", p=P)).then_inc(x_in_sem[b], 16)
                if b == 0:
                    sp.dma_start(wqkv[:, :], wqkv_in).then_inc(wqkv_in_sem, 16)
            sp.dma_start(wo[:, :], wo_in).then_inc(w_in, 16)
            sp.dma_start(wg[:, :], wg_in).then_inc(w_in, 16)

            def parts(b):
                sp.wait_ge(lo_ready, 4 * (b + 1))
                for w, (dram, order) in enumerate(((q_dram, Q_PART), (k_dram, K_PART))):
                    for r in range(TERMS):
                        sp.dma_start(
                            dram[b * NH:(b + 1) * NH, r * HD:(r + 1) * HD, :],
                            part[w][order[r]][:, b * S:(b + 1) * S]).then_inc(parts_out, 16)

            def load(s, dst_q, dst_k, par, done):
                for jj in range(2):
                    sp.dma_start(dst_q[64 * jj:64 * jj + KR, par, :, :],
                                 q_dram[bass.ds(s * G + jj, 2, step=2)].rearrange("a r n -> r a n")).then_inc(done, 16)
                    sp.dma_start(dst_k[64 * jj:64 * jj + KR, par, jj::2, :],
                                 k_dram[bass.ds(s * G + jj, 2, step=2)].rearrange("a r n -> r a n")).then_inc(done, 16)

            def load_piece(n):
                k, e = W_PIECES[n]
                if n >= 2:
                    sp.wait_ge(w_lo, n - 1)
                if k < 2:
                    sp.dma_start(wst[:, n % 2, 0:FH],
                                 (w1_in, w3_in)[k][:, e * FH:(e + 1) * FH]).then_inc(w_stage[n % 2], 32)
                else:
                    v = wst[:, n % 2, :].rearrange("p (c d) -> p c d", c=FC)
                    sp.dma_start(v[:, 0:FC - 1, :],
                                 w2_in[e, 0:(FC - 1) * P, :].rearrange("(c p) d -> p c d", p=P)).then_inc(w_stage[n % 2], 16)
                    sp.dma_start(v[0:TAIL, FC - 1, :], w2_in[e, (FC - 1) * P:FH, :]).then_inc(w_stage[n % 2], 16)

            for n in range(6):
                load_piece(n)
            parts(0)
            sp.wait_ge(op_zero, 4)
            sp.wait_ge(kb_one, 2)
            sp.wait_ge(parts_out, 16 * 2 * TERMS)
            load(0, qa, ka, 0, a_loaded[0])
            load(0, qb, kb, 0, b_loaded[0])
            parts(1)
            sp.wait_ge(pool_const, 1)
            sp.dma_start(xs_dram.rearrange("(p t) d -> p t d", t=TILES),
                         zrow[:, :].rearrange("p (o d) -> p o d", o=1).to_broadcast([P, TILES, 2 * D])).then_inc(xs_zero, 16)
            for n in range(6, NW):
                load_piece(n)
            sp.wait_ge(parts_out, 16 * 2 * TERMS * NB)
            sp.wait_ge(w_lo, NW)
            sp.wait_ge(w_hi, NW)
            sp.wait_ge(tile_e_ready, 1)

            def store_y(s, k):
                T = first_tile(s)[0] + k
                sp.wait_ge(ey_ready, T + 1)
                sp.dma_start(y_dram[bass.ds(T * P, P), :], ysb[:, parity(s, k), :]).then_inc(ey_out[parity(s, k)], 16)

            def step(s, par, do_a):
                if do_a:
                    if not known(s, 1):
                        sp.wait_ge(a_scores, NA * (s - 1))
                    load(s, qa, ka, par, a_loaded[par])
                if not known(s, 1):
                    before_n = FIRST if known(s, 2) else 6
                    T = first_tile(s)[0]
                    for k in (-2, -1):
                        sp.wait_ge(ey_ready, T + k + 1)
                        q = (k + FIRST) % 2
                        sp.dma_start(y_dram[bass.ds((T + k) * P, P), :], ysb[:, q, :]).then_inc(ey_out[q], 16)
                if not do_a:
                    return
                if not known(s, 1):
                    sp.wait_ge(b_scores, NBU * (s - 1))
                load(s, qb, kb, par, b_loaded[par])
                T, n = first_tile(s)
                for k in range(n):
                    q = parity(s, k)
                    if not (known(s, 1) and k < 2):
                        sp.wait_ge(xsT_done, T + k - 1)
                    if known(s, 1) and k == 0:
                        sp.wait_ge(scattered, 16 * 2 * NT)
                    e = sp.value_load(tile_e[0:1, bass.ds(T + k, 1)], min_val=0, max_val=E - 1)
                    sp.dma_start(xs[:, q, :], xs_dram[bass.ds((T + k) * P, P), :]).then_inc(x_here[q], 16)
                    if not (known(s, 1) and k < 2):
                        sp.wait_ge(ey_done, T + k - 1)
                    sp.dma_start(wbuf[:, q, :], wall[:, bass.ds(e, 1), :].rearrange("p e w -> p (e w)")).then_inc(w_here[q], 16)
                    if k >= 2:
                        store_y(s, k - 2)

            step(1, 1, True)
            with sp.Fori(1, ITS // 2) as i:
                step(2 * i, 0, True)
                step(2 * i + 1, 1, True)
            step(ITS, 0, False)

            for c in range(NT // 4):
                b, t0 = c // 2, 4 * (c % 2)
                sp.wait_ge(combined, 8 * (c + 1))
                sp.dma_start(out[b].rearrange("(t p) d -> p t d", p=P)[:, t0:t0 + 4, :],
                             x[:, 4 * c:4 * c + 4, :]).then_inc(out_done, 16)
            sp.wait_ge(out_done, 16 * NT // 4)

        @block.gpsimd
        def _(pool):
            pool.memset(zrow[:, :], 0.0).then_inc(pool_const, 1)
            pool.memset(identf[:, :], 0.0).then_inc(pool_const, 1)
            pool.memset(identb[:, :], 0.0).then_inc(pool_const, 1)
            pool.memset(causal[:, :], 0.0).then_inc(pool_const, 1)
            pool.memset(before[:, :], 1.0).then_inc(pool_const, 1)
            pool.memset(onesb[:, :], 1.0).then_inc(pool_const, 1)
            pool.memset(lower[:, :, :], 1.0).then_inc(pool_const, 1)
            pool.wait_ge(pool_const, 7)
            pool.affine_select(out=identf[:, :], in_=identf[:, :], compare_op=ALU.not_equal, fill=1.0,
                               base=0, pattern=[[-1, P]], channel_multiplier=1).then_inc(pool_const, 1)
            pool.affine_select(out=identb[:, :], in_=identb[:, :], compare_op=ALU.not_equal, fill=1.0,
                               base=0, pattern=[[-1, P]], channel_multiplier=1).then_inc(pool_const, 1)
            pool.affine_select(out=causal[:, CH - P:CH], in_=causal[:, CH - P:CH], compare_op=ALU.is_ge, fill=NEG,
                               base=0, pattern=[[-1, P]], channel_multiplier=1).then_inc(pool_const, 1)
            pool.affine_select(out=before[:, :], in_=before[:, :], compare_op=ALU.is_gt, fill=0.0,
                               base=0, pattern=[[1, P]], channel_multiplier=-1).then_inc(pool_const, 1)
            pool.affine_select(out=lower[:, :, :], in_=lower[:, :, :], compare_op=ALU.is_gt, fill=0.0,
                               base=0, pattern=[[1, E], [-1, E]], channel_multiplier=0).then_inc(pool_const, 1)
            pool.iota(iota_e[:, :], pattern=[[1, E]], base=0, channel_multiplier=0,
                      allow_small_or_imprecise_dtypes=True).then_inc(pool_const, 1)
            pool.iota(iota_t[:, :], pattern=[[1, TILES]], base=0, channel_multiplier=0,
                      allow_small_or_imprecise_dtypes=True).then_inc(pool_const, 1)
            pool.iota(iota_s[:, :], pattern=[[P, NT]], base=0, channel_multiplier=0,
                      allow_small_or_imprecise_dtypes=True).then_inc(pool_const, 1)
            for k in range(3):
                for i in range(2):
                    pad = slice(FH, HP) if k < 2 else slice((FC - 1) * P, HP)
                    pool.memset(wall[:, :, (2 * k + i) * HP + pad.start:(2 * k + i) * HP + pad.stop], 0.0).then_inc(pad_zero, 1)
            for t in (qa, ka, qb, kb):
                pool.memset(t[:, :, :, :], 0.0).then_inc(op_zero, 1)
            pool.wait_ge(op_zero, 4)
            pool.memset(kb[32:64, :, 0::2, :], 1.0).then_inc(kb_one, 1)
            pool.wait_ge(kb_one, 1)
            pool.memset(kb[96:128, :, 1::2, :], 1.0).then_inc(kb_one, 1)
            pool.wait_ge(kb_one, 2)
            pool.memset(mpart[:, :, :, :, :], NEG).then_inc(pool_const, 1)
            pool.memset(vw[:, :, :, :, :], 0.0).then_inc(pool_const, 1)
            pool.wait_ge(pool_const, 17)
            pool.memset(vw[:, :, :, :, HD:HD + 1], 1.0).then_inc(pool_const, 1)

            pool.wait_ge(pad_zero, 6)
            for n, (k, e) in enumerate(W_PIECES):
                pool.wait_ge(w_hi, n + 1)
                areas = w_areas(k)
                for m, (rows, cols) in enumerate(areas):
                    if m:
                        pool.wait_ge(w_tail, n // 3 + 1)
                    last = pool.tensor_tensor(w_part(wall[rows, e, :], k, 1, cols), wst[rows, n % 2, cols],
                                              w_part(wall[rows, e, :], k, 0, cols), ALU.subtract)
                    if m < len(areas) - 1:
                        last.then_inc(w_tail, 1)
                last.then_inc(w_lo, 1)
                pool.wait_ge(w_lo, n + 1)
                if n % 6 == 5:
                    c = n // 6
                    pool.wait_ge(xhi_ready, c + 1)
                    pool.tensor_tensor(xhl[:, 4 * c:4 * c + 4, 1, :], xn[:, 4 * c:4 * c + 4, :],
                                       xhl[:, 4 * c:4 * c + 4, 0, :], ALU.subtract).then_inc(xlo_ready, 1)
            pool.wait_ge(xlo_ready, NT // 4)
            pool.wait_ge(pos_ready, 1)
            pool.wait_ge(xs_zero, 16)
            for k in range(2):
                for t in range(NT):
                    pool.indirect_dma_start(
                        out=xs_dram, out_offset=bass.IndirectOffsetOnAxis(ap=pos[:, k, t:t + 1], axis=0),
                        in_=xhl[:, t, :, :].rearrange("p a d -> p (a d)"), in_offset=None).then_inc(scattered, 16)
            pool.wait_ge(v_ready, NT // 4)

            def step(s, par, do_a, do_b):
                if do_a:
                    if do_b and not known(s, 1):
                        pool.wait_ge(pv_done, NS * (s - 1))
                    pool.tensor_copy(vw[:, par, :, :, 0:HD],
                                     vall[:, bass.ds(s, 1), :, :].rearrange("p a k (j d) -> p (a k) j d", j=G)).then_inc(vw_ready, 1)
                if do_b:
                    for n, (c, k) in enumerate(B_STEPS):
                        if k * P >= c * CH:
                            pool.wait_ge(exp_done, NBU * (s - 1) + G * (n + 1))
                            pool.sem_inc(pool_passed, 1)
                            v = prob[:, n % PSLOTS, :, 0:P]
                            pool.affine_select(out=v, in_=v, compare_op=ALU.is_ge, fill=0.0, base=0,
                                               pattern=[[0, G], [1, P]], channel_multiplier=-1).then_inc(masked, 1)
                if do_a and do_b:
                    T, n = first_tile(s)
                    for k in range(n):
                        pool.wait_ge(hh_ready, T + k + 1)
                        if not (known(s, 1) and k == 0):
                            pool.wait_ge(ey_done, T + k)
                        pool.tensor_tensor(hl[:, :], hf[:, :], hh[:, :], ALU.subtract).then_inc(hl_ready, 1)

            step(0, 0, True, False)
            step(1, 1, True, True)
            with pool.Fori(1, ITS // 2) as i:
                step(2 * i, 0, True, True)
                step(2 * i + 1, 1, True, True)
            for q in range(2):
                pool.wait_ge(ey_out[q], 16 * ((TILES + 1 - q) // 2))
            step(ITS, 0, False, True)
            for t in range(NT):
                for k in range(2):
                    pool.indirect_dma_start(
                        out=yg[:, k, t, :], out_offset=None, in_=y_dram,
                        in_offset=bass.IndirectOffsetOnAxis(ap=pos[:, k, t:t + 1], axis=0)).then_inc(gathered[t // 4], 16)

        @block.scalar
        def _(act):
            pieces = iter(range(NW))

            def piece():
                n = next(pieces, None)
                if n is None:
                    return
                k, e = W_PIECES[n]
                if n == 0:
                    act.wait_ge(pad_zero, 6)
                act.wait_ge(w_stage[n % 2], 32 * (n // 2 + 1))
                for rows, cols in w_areas(k):
                    last = act.activation(w_part(wall[rows, e, :], k, 0, cols), wst[rows, n % 2, cols], ACT.Copy)
                last.then_inc(w_hi, 1)

            for b in range(NB):
                act.wait_ge(veps_ready, b + 1)
                act.activation(sdev[:, b * TB:(b + 1) * TB], veps[:, b * TB:(b + 1) * TB], ACT.Sqrt).then_inc(sdev_ready, 1)

            def turned(c):
                act.wait_ge(xT_done, c + 1)
                act.activation(xnT[:, c * CH:(c + 1) * CH], bank[c % 2][:, :], ACT.Copy).then_inc(xnT_ready, 1)

            def hi(n):
                w, c = n % 2, n // 2
                act.wait_ge(qk_proj, n + 1)
                act.activation(part[w][0][:, c * CH:(c + 1) * CH], ps_b[n % 2][:, :], ACT.Copy).then_inc(hi_ready, 1)

            def mid(n):
                w, c = n % 2, n // 2
                act.wait_ge(rest_ready, n + 1)
                act.activation(part[w][1][:, c * CH:(c + 1) * CH], rest[:, n % 2, :], ACT.Copy).then_inc(mid_ready, 1)

            for c in range(NT // 4):
                turned(c)
                hi(2 * c)
                if c:
                    mid(2 * c - 1)
                hi(2 * c + 1)
                mid(2 * c)
                act.activation(xhl[:, 4 * c:4 * c + 4, 0, :], xn[:, 4 * c:4 * c + 4, :], ACT.Copy).then_inc(xhi_ready, 1)
            mid(2 * (NT // 4) - 1)
            act.wait_ge(ex_in, 1)
            act.activation(sc[:, :, :], lg[:, :, :], ACT.Exp).then_inc(ex_ready, 1)
            for c in range(NT // 4):
                act.wait_ge(v_proj, c + 1)
                b, k0 = c // 2, 4 * (c % 2)
                for k in range(4):
                    last = act.activation(vall[:, b * NG:(b + 1) * NG, k0 + k, :],
                                          ps_b[2][:, k * P:(k + 1) * P].rearrange("p (g d) -> p g d", g=NG) if c % 2
                                          else ps_a[2][:, k * P:(k + 1) * P].rearrange("p (g d) -> p g d", g=NG), ACT.Copy)
                last.then_inc(v_ready, 1)
            for _ in range(NW):
                piece()

            def o_copy(s, c):
                act.wait_ge(pv_done, NS * (s - 1) + (G if c == 0 else NS))
                if not (known(s, 1) and c == 0):
                    act.wait_ge(oT_done, 2 * (s - 1) + c)
                act.activation(osb[:, :], ps_o[:, :], ACT.Copy).then_inc(osb_ready, 1)

            def m_copy(s):
                act.wait_ge(mT_done, s + 1)
                if not known(s, 0):
                    act.wait_ge(m_loaded, 64 * s)
                act.activation(mrow[:, :], ps_m16[0:3 * G, :], ACT.Copy).then_inc(mrow_ready, 1)
                act.wait_ge(mrow_ready, s + 1)
                if not known(s, 0, 1):
                    act.wait_ge(b_scores, NBU * (s - 1))
                for j in range(G):
                    r = 64 * (j % 2) + KR
                    act.dma_start(qb[r:r + 3, 0 if known(s, 0) else s_par[0], j // 2, :],
                                  mrow[3 * j:3 * j + 3, :]).then_inc(m_loaded, 16)

            s_par = [0]

            def step(s, par, do_a, do_b):
                s_par[0] = par
                for n in range(NS if do_b else 0):
                    N = CH - b_first(n)
                    for j in range(G):
                        u = n * G + j
                        act.wait_ge(b_scores, NBU * (s - 1) + u + 1)
                        if j == 0 and not (known(s, 1) and n < PSLOTS):
                            act.wait_ge(pv_done, NS * (s - 1) + n - PSLOTS + 1)
                        act.activation(prob[:, n % PSLOTS, j, 0:N], ps_b[u % RING][:, 0:N],
                                       ACT.Exp, scale=SCALE).then_inc(exp_done, 1)
                    if n == O_COPY:
                        o_copy(s, 0)
                if not (do_a and do_b):
                    if do_b:
                        o_copy(s, 1)
                    if do_a:
                        m_copy(s)
                    return
                T, tiles = first_tile(s)

                def x_copy(k):
                    act.wait_ge(xsT_done, T + k + 1)
                    if not (known(s, 1) and k < 2):
                        act.wait_ge(h_done, T + k - 1)
                    act.activation(xsT[:, parity(s, k), :], ps_x[:, 0:2 * D], ACT.Copy).then_inc(xsT_ready, 1)

                def y_copy(k):
                    act.wait_ge(ey_done, T + k + 1)
                    q = parity(s, k)
                    if not (known(s, 1) and k < 2):
                        act.wait_ge(ey_out[q], tile_loads(s, k) - 16)
                    act.activation(ysb[:, q, :], ps_y[:, 0:D], ACT.Copy).then_inc(ey_ready, 1)

                x_copy(0)
                for k in range(tiles):
                    act.wait_ge(h_done, T + k + 1)
                    if not (known(s, 1) and k == 0):
                        act.wait_ge(ha_ready, T + k)
                    act.activation(th[:, :], ps_h[parity(s, k)][0][:, 0:HP], ACT.Tanh, scale=0.5).then_inc(th_ready, 1)
                    if k + 1 < tiles:
                        x_copy(k + 1)
                    if k == 0:
                        o_copy(s, 1)
                    else:
                        y_copy(k - 1)
                    act.wait_ge(hf_ready, T + k + 1)
                    if not (known(s, 1) and k == 0):
                        act.wait_ge(ey_done, T + k)
                    act.activation(hh[:, :], hf[:, :], ACT.Copy).then_inc(hh_ready, 1)
                    if k == 1:
                        m_copy(s)
                y_copy(tiles - 1)

            step(0, 0, True, False)
            step(1, 1, True, True)
            with act.Fori(1, ITS // 2) as i:
                step(2 * i, 0, True, True)
                step(2 * i + 1, 1, True, True)
            step(ITS, 0, False, True)

        @block.vector
        def _(v):
            chain = [0]

            def link(ins):
                chain[0] += 1
                ins.then_inc(dve, 1)
                v.wait_ge(dve, chain[0])

            for b in range(NB):
                v.wait_ge(x_in_sem[b], 16)
                for t in range(b * TB, (b + 1) * TB):
                    last = v.bn_stats(stats[:, t, :], x[:, t, :])
                link(last)
                for t in range(b * TB, (b + 1) * TB):
                    last = v.bn_aggr(mv[:, t, :], stats[:, t, :])
                link(last)
                v.tensor_scalar(veps[:, b * TB:(b + 1) * TB], mv[:, b * TB:(b + 1) * TB, 1], 1e-5, None,
                                ALU.add).then_inc(veps_ready, 1)
            for b in range(NB):
                v.wait_ge(sdev_ready, b + 1)
                link(v.reciprocal(rstd[:, b * TB:(b + 1) * TB], sdev[:, b * TB:(b + 1) * TB]))
                for t in range(b * TB, (b + 1) * TB):
                    v.tensor_scalar(xn[:, t, :], x[:, t, :], mv[:, t, 0:1], rstd[:, t:t + 1],
                                    ALU.subtract, ALU.mult).then_inc(xn_ready, 1)
            for n in range(2 * NT // 4 + 1):
                if n < 2 * NT // 4:
                    w, c = n % 2, n // 2
                    v.wait_ge(hi_ready, n + 1)
                    if n >= 2:
                        v.wait_ge(lo_ready, n - 1)
                    v.tensor_tensor(rest[:, n % 2, :], ps_b[n % 2][:, :], part[w][0][:, c * CH:(c + 1) * CH],
                                    ALU.subtract).then_inc(rest_ready, 1)
                if n >= 1:
                    w, c = (n - 1) % 2, (n - 1) // 2
                    v.wait_ge(mid_ready, n)
                    v.tensor_tensor(part[w][2][:, c * CH:(c + 1) * CH], rest[:, (n - 1) % 2, :],
                                    part[w][1][:, c * CH:(c + 1) * CH], ALU.subtract).then_inc(lo_ready, 1)
            v.wait_ge(logits_done, 1)
            lps = ps_m[:, 0:NT * E].rearrange("p (t e) -> p t e", e=E)
            link(v.tensor_reduce(r1[:, :], lps, AX_X, ALU.max))

            def rows(a, n=E):
                return a.rearrange("p (t o) -> p t o", o=1).to_broadcast([P, a.shape[1], n])

            def cols(a, n):
                return a.rearrange("p (o e) -> p o e", o=1).to_broadcast([P, n, a.shape[1]])

            v.tensor_tensor(lg[:, :, :], lps, rows(r1[:, :]), ALU.subtract).then_inc(ex_in, 1)
            v.wait_ge(ex_ready, 1)
            link(v.tensor_reduce(r1[:, :], sc[:, :, :], AX_X, ALU.add))
            link(v.reciprocal(r2[:, :], r1[:, :]))
            link(v.tensor_tensor(lg[:, :, :], sc[:, :, :], rows(r2[:, :]), ALU.mult))
            for t in range(NT):
                last = v.max(top[:, t, :], lg[:, t, :])
            link(last)
            for t in range(NT):
                last = v.max_index(topi[:, t, :], top[:, t, :], lg[:, t, :])
            link(last)
            link(v.tensor_copy(topf[:, :, :], topi[:, :, :]))
            v.wait_ge(pool_const, 18)
            for k in range(2):
                last = v.tensor_tensor(hot[:, k, :, :], cols(iota_e[:, :], NT), rows(topf[:, :, k]), ALU.is_equal)
            link(last)
            v.tensor_tensor(both[:, :, :], hot[:, 0, :, :], hot[:, 1, :, :], ALU.add).then_inc(both_ready, 1)
            link(v.tensor_tensor(r1[:, :], top[:, :, 0], top[:, :, 1], ALU.add))
            link(v.tensor_scalar(r1[:, :], r1[:, :], 1e-20, None, ALU.add))
            link(v.reciprocal(r2[:, :], r1[:, :]))
            for k in range(2):
                last = v.tensor_tensor(gate[:, k, :], top[:, :, k], r2[:, :], ALU.mult)
            link(last)
            v.wait_ge(rank_done, 1)
            rank = ps_m[:, 0:NT * E].rearrange("p (t e) -> p t e", e=E)
            count = ps_m[:, NT * E:NT * E + E]
            big16 = big[:, 0:2 * E, :].rearrange("p a b -> p (a b)").rearrange("p (e s) -> p e s", e=E)
            link(v.tensor_tensor(big16, rows(count, NT), cols(iota_s[:, :], E), ALU.is_gt))
            link(v.tensor_reduce(ntile[:, :], big16, AX_X, ALU.add))
            link(v.tensor_tensor(big[:, 0:E, :], lower[:, :, :], cols(ntile[:, :], E), ALU.mult))
            link(v.tensor_reduce(start[:, :], big[:, 0:E, :], AX_X, ALU.add))
            link(v.tensor_tensor(big[:, :, :], cols(start[:, :], TILES), rows(iota_t[:, :]), ALU.is_le))
            link(v.tensor_reduce(tile_f[:, :], big[:, :, :], AX_X, ALU.add))
            v.tensor_scalar(tile_e[:, :], tile_f[:, :], -1.0, None, ALU.add).then_inc(tile_e_ready, 1)
            link(v.tensor_scalar(start[:, :], start[:, :], float(P), None, ALU.mult))
            v.tensor_tensor(lg[:, :, :], rank, cols(start[:, :], NT), ALU.add).then_inc(rank_read, 1)
            v.wait_ge(rank_read, 1)
            for k in range(2):
                link(v.tensor_tensor(sc[:, :, :], lg[:, :, :], hot[:, k, :, :], ALU.mult))
                link(v.tensor_reduce(posf[:, k, :], sc[:, :, :], AX_X, ALU.add))
            v.tensor_copy(pos[:, :, :], posf[:, :, :]).then_inc(pos_ready, 1)

            def row_max(s, par, u):
                i, j, c = A_UNITS[u]
                N = a_cols(u)
                v.wait_ge(a_scores, NA * s + u + 1)
                dst = mpart[:, par, i, j, c:c + 1]
                if (i + 1) * P <= c * CH + CH:
                    v.sem_inc(dve_passed, 1)
                    v.tensor_tensor_reduce(junk[:, u % RING, 0:N], ps_a[u % RING][:, 0:N], causal[:, CH - N:CH], 1.0, NEG,
                                           ALU.add, ALU.max, dst).then_inc(a_used, 1)
                else:
                    v.tensor_reduce(dst, ps_a[u % RING][:, 0:N], AX_X, ALU.max).then_inc(a_used, 1)

            def split_max(s, par):
                v.wait_ge(a_used, NA * (s + 1))
                if not known(s, 0):
                    v.wait_ge(mT_done, s)
                v.tensor_reduce(nmax[:, :, :], mpart[:, par, :, :, :], AX_X, ALU.max, negate=True).then_inc(max_chain, 1)
                v.wait_ge(max_chain, 5 * s + 1)
                v.tensor_copy(mt[:, :, :, 0], nmax[:, :, :]).then_inc(max_chain, 1)
                v.wait_ge(max_chain, 5 * s + 2)
                v.tensor_tensor(nmr[:, 0, :, :], nmax[:, :, :], mt[:, :, :, 0], ALU.subtract).then_inc(max_chain, 1)
                v.wait_ge(max_chain, 5 * s + 3)
                v.tensor_copy(mt[:, :, :, 1], nmr[:, 0, :, :]).then_inc(max_chain, 1)
                v.wait_ge(max_chain, 5 * s + 4)
                v.tensor_tensor(nmr[:, 1, :, :], nmr[:, 0, :, :], mt[:, :, :, 1], ALU.subtract).then_inc(max_chain, 1)
                v.wait_ge(max_chain, 5 * s + 5)
                v.tensor_copy(mt[:, :, :, 2], nmr[:, 1, :, :]).then_inc(mt_ready, 1)

            def normalise(s, c):
                v.wait_ge(oT_done, 2 * (s - 1) + c + 1)
                if not (known(s, 1) and c == 0):
                    v.wait_ge(attn_ready, 2 * (s - 1) + c)
                o = ps_m[:, :].rearrange("p (t j d) -> p t j d", t=4, j=G)
                v.reciprocal(rden[:, :, :], o[:, :, :, HD]).then_inc(rden_ready, 1)
                v.wait_ge(rden_ready, 2 * (s - 1) + c + 1)
                dst = attn[:, bass.ds((s - 1) // NG, 1), 4 * c:4 * c + 4, bass.ds((s - 1) % NG, 1), :]
                v.tensor_tensor(dst.rearrange("p a t g (j d) -> p (a t g) j d", j=G), o[:, :, :, 0:HD],
                                rden[:, :, :].rearrange("p t (j o) -> p t j o", o=1).to_broadcast([P, 4, G, HD]),
                                ALU.mult).then_inc(attn_ready, 1)

            def step(s, par, do_a, do_b):
                for n in range(NS):
                    if do_a:
                        for u in a_slots[n]:
                            row_max(s, par, u)
                    if n == O_TURN and do_b:
                        normalise(s, 0)
                if do_a:
                    split_max(s, par)
                if do_a and do_b:
                    T, tiles = first_tile(s)
                    for k in range(tiles):
                        h1, h3 = ps_h[parity(s, k)]
                        v.wait_ge(th_ready, T + k + 1)
                        if not (known(s, 1) and k == 0):
                            v.wait_ge(hf_ready, T + k)
                        v.scalar_tensor_tensor(out=ha[:, :], in0=th[:, :], scalar=1.0, in1=h1[:, 0:HP],
                                               op0=ALU.add, op1=ALU.mult).then_inc(ha_ready, 1)
                        v.wait_ge(ha_ready, T + k + 1)
                        if not (known(s, 1) and k == 0):
                            v.wait_ge(hl_ready, T + k)
                        v.scalar_tensor_tensor(out=hf[:, :], in0=ha[:, :], scalar=0.5, in1=h3[:, 0:HP],
                                               op0=ALU.mult, op1=ALU.mult).then_inc(hf_ready, 1)
                        if k == 1:
                            normalise(s, 1)
                elif do_b:
                    normalise(s, 1)

            step(0, 0, True, False)
            step(1, 1, True, True)
            with v.Fori(1, ITS // 2) as i:
                step(2 * i, 0, True, True)
                step(2 * i + 1, 1, True, True)
            step(ITS, 0, False, True)

            yT = prob[:, 0, :, 0:P]
            for c in range(NT // 4):
                v.wait_ge(yT_done, c + 1)
                if c >= 1:
                    v.wait_ge(y_done, c)
                v.tensor_copy(yT, ps_a[c % 2][:, :].rearrange("p (t d) -> p t d", t=4)).then_inc(yT_ready, 1)
                v.wait_ge(y_done, c + 1)
                v.tensor_tensor(x[:, 4 * c:4 * c + 4, :], ps_b[c % 2][:, :].rearrange("p (t d) -> p t d", t=4),
                                x[:, 4 * c:4 * c + 4, :], ALU.add).then_inc(y_added, 1)
            v.wait_ge(y_added, NT // 4)
            for t in range(NT):
                if t % 4 == 0:
                    v.wait_ge(gathered[t // 4], 16 * 8)
                for k in range(2):
                    if k:
                        v.wait_ge(combined, 2 * t + 1)
                    v.scalar_tensor_tensor(out=x[:, t, :], in0=yg[:, k, t, :], scalar=gate[:, k, t:t + 1],
                                           in1=x[:, t, :], op0=ALU.mult, op1=ALU.add).then_inc(combined, 1)

        @block.tensor
        def _(pe):
            pe.wait_ge(pool_const, 15)
            for t in range(NT):
                c = t // 4
                pe.wait_ge(xn_ready, t + 1)
                if c >= 2 and t % 4 == 0:
                    pe.wait_ge(xnT_ready, c - 1)
                last = pe.transpose(bank[c % 2][:, (t % 4) * P:(t % 4 + 1) * P], xn[:, t, :], identf[:, :])
                if t % 4 == 3:
                    last.then_inc(xT_done, 1)
                    if c == 0:
                        pe.wait_ge(wqkv_in_sem, 16)
                    pe.wait_ge(xnT_ready, c + 1)
                    for n in (2 * c, 2 * c + 1):
                        w = n % 2
                        if n >= 2:
                            pe.wait_ge(rest_ready, n - 1)
                        pe.matmul(ps_b[n % 2][:, :], wqkv[:, w * D:(w + 1) * D], xnT[:, c * CH:(c + 1) * CH],
                                  start=True, stop=True).then_inc(qk_proj, 1)
            pe.wait_ge(w_in, 32)
            for t in range(NT):
                last = pe.matmul(ps_m[:, t * E:(t + 1) * E], xnT[:, t * P:(t + 1) * P], wg[:, :], start=True, stop=True)
            last.then_inc(logits_done, 1)
            for t in range(NT):
                c = t // 4
                if c >= 2 and t % 4 == 0:
                    pe.wait_ge(v_ready, c - 1)
                last = pe.matmul((ps_b[2] if c % 2 else ps_a[2])[:, (t % 4) * P:(t % 4 + 1) * P], xnT[:, t * P:(t + 1) * P],
                                 wqkv[:, 2 * D:3 * D], start=True, stop=True)
                if t % 4 == 3:
                    last.then_inc(v_proj, 1)
            pe.wait_ge(both_ready, 1)
            for t in range(NT):
                last = pe.matmul(ps_m[:, NT * E:NT * E + E], onesb[:, :], both[:, t, :], start=(t == 0), stop=(t == NT - 1))
            pe.matmul(ps_m[:, 0:E], before[:, :], both[:, 0, :], start=True, stop=True)
            pe.matmul(ps_m[:, E:NT * E], before[:, :], both[:, 1:NT, :].rearrange("p t e -> p (t e)"),
                      start=True, stop=False, skip_group_check=True)
            for t in reversed(range(NT - 1)):
                later = both[:, t, :].rearrange("p (o e) -> p o e", o=1).to_broadcast([P, NT - 1 - t, E])
                last = pe.matmul(ps_m[:, (t + 1) * E:NT * E], onesb[:, :], later, start=False, stop=(t == 0),
                                 skip_group_check=True)
            last.then_inc(rank_done, 1)
            pe.wait_ge(v_ready, NT // 4)
            pe.wait_ge(rest_ready, 2 * NT // 4)

            def a_unit(s, par, u):
                i, j, c = A_UNITS[u]
                N = a_cols(u)
                if u == 0:
                    pe.wait_ge(a_loaded[par], 4 * loads(s, par))
                if not (known(s, 0) and u < RING):
                    pe.wait_ge(a_used, NA * s + u + 1 - RING)
                pe.matmul(ps_a[u % RING][:, 0:N], qa[:, par, j // 2, i * P:(i + 1) * P],
                          ka[:, par, j, c * CH:c * CH + N], start=True, stop=True).then_inc(a_scores, 1)

            def b_unit(s, par, u):
                n, j = u // G, u % G
                c, k = B_STEPS[n]
                q0 = b_first(n)
                if u == 0:
                    pe.wait_ge(b_loaded[par], 4 * loads(s, par))
                    pe.wait_ge(m_loaded, 64 * (s + 1))
                if not (known(s, 0) and u < RING):
                    pe.wait_ge(exp_done, NBU * s + u + 1 - RING)
                pe.matmul(ps_b[u % RING][:, 0:CH - q0], kb[:, par, j, k * P:(k + 1) * P],
                          qb[:, par, j // 2, c * CH + q0:(c + 1) * CH], start=True, stop=True).then_inc(b_scores, 1)

            def pv(s, par, n):
                c, k = B_STEPS[n]
                q0 = b_first(n)
                pe.wait_ge(exp_done, NBU * s + G * (n + 1))
                if k * P >= c * CH:
                    pe.wait_ge(masked, DIAG * s + (k + 1))
                if n == 0:
                    pe.wait_ge(vw_ready, s + 1)
                if k == 0 and not (known(s, 0) and c == 0):
                    pe.wait_ge(osb_ready, 2 * s + c)
                for j in range(G):
                    last = pe.matmul(ps_o[32 * j:32 * j + 32, q0:CH], vw[:, par, k, j, :],
                                     prob[:, n % PSLOTS, j, 0:CH - q0], start=(k == 0),
                                     stop=(k == (c + 1) * CH // P - 1), skip_group_check=True)
                last.then_inc(pv_done, 1)

            def o_turn(s, c):
                pe.wait_ge(osb_ready, 2 * s + c + 1)
                if c == 0:
                    pe.wait_ge(mrow_ready, s + 1)
                else:
                    pe.wait_ge(attn_ready, 2 * s + c)
                for t in range(4):
                    last = pe.transpose(ps_m[:, t * P:(t + 1) * P], osb[:, t * P:(t + 1) * P], identf[:, :])
                last.then_inc(oT_done, 1)

            def m_turn(s):
                pe.wait_ge(mt_ready, s + 1)
                if known(s, 0):
                    pe.wait_ge(rank_read, 1)
                else:
                    pe.wait_ge(attn_ready, 2 * s)
                for i in range(TB):
                    last = pe.transpose(ps_m16[0:3 * G, i * P:(i + 1) * P],
                                        mt[:, i, :, :].rearrange("p j r -> p (j r)"), identb[:, :])
                last.then_inc(mT_done, 1)

            PASSES = ((0, 0), (1, 0), (0, 1))

            def step(s, par, do_a, do_b):
                for n in range(NS):
                    mine = [u for u in a_slots[n]] if do_a else []
                    for j in range(G):
                        if do_b:
                            b_unit(s - 1, 1 - par, n * G + j)
                        if mine:
                            a_unit(s, par, mine.pop(0))
                    for u in mine:
                        a_unit(s, par, u)
                    if do_b and n >= LAG:
                        pv(s - 1, 1 - par, n - LAG)
                    if do_b and n == O_TURN:
                        o_turn(s - 1, 0)
                if not (do_a and do_b):
                    if do_b:
                        for n in range(NS - LAG, NS):
                            pv(s - 1, 1 - par, n)
                        o_turn(s - 1, 1)
                    if do_a:
                        m_turn(s)
                    return
                T, tiles = first_tile(s)

                def x_turn(k):
                    q = parity(s, k)
                    pe.wait_ge(x_here[q], tile_loads(s, k))
                    if k == 0:
                        pe.wait_ge(a_used, NA * (s + 1))
                    else:
                        pe.wait_ge(xsT_ready, T + k)
                    for i in range(2):
                        last = pe.transpose(ps_x[:, i * D:(i + 1) * D], xs[:, q, i * D:(i + 1) * D], identb[:, :])
                    last.then_inc(xsT_done, 1)

                def hidden(k):
                    q = parity(s, k)
                    pe.wait_ge(w_here[q], tile_loads(s, k))
                    pe.wait_ge(xsT_ready, T + k + 1)
                    if k == 1:
                        pe.wait_ge(exp_done, NBU * s)
                    if k == 0:
                        pe.wait_ge(a_used, NA * (s + 1))
                        pe.wait_ge(exp_done, NBU * s)
                    if k >= 2:
                        pe.wait_ge(hf_ready, T + k - 1)
                    for w in range(2):
                        for f in range(FC):
                            for i, (a, b) in enumerate(PASSES):
                                cols = slice(f * P, (f + 1) * P)
                                last = pe.matmul(ps_h[q][w][:, cols], w_part(wbuf[:, q, :], w, a, cols),
                                                 xsT[:, q, b * D:(b + 1) * D], start=(i == 0), stop=(i == 2))
                    last.then_inc(h_done, 1)

                def down(k):
                    q = parity(s, k)
                    pe.wait_ge(hl_ready, T + k + 1)
                    if k:
                        pe.wait_ge(ey_ready, T + k)
                    for i, (a, b) in enumerate(PASSES):
                        for f in range(FC):
                            cols = slice(f * P, (f + 1) * P)
                            last = pe.matmul(ps_y[:, 0:D], (hh, hl)[b][:, cols], w_part(wbuf[:, q, :], 2, a, cols),
                                             start=(i == 0 and f == 0), stop=(i == 2 and f == FC - 1))
                    last.then_inc(ey_done, 1)

                for n in range(NS - LAG, NS - 1):
                    pv(s - 1, 1 - par, n)
                x_turn(0)
                for k in range(tiles):
                    hidden(k)
                    if k + 1 < tiles:
                        x_turn(k + 1)
                    if k == 0:
                        pv(s - 1, 1 - par, NS - 1)
                    else:
                        down(k - 1)
                    if k == 1:
                        o_turn(s - 1, 1)
                        m_turn(s)
                down(tiles - 1)
                pe.wait_ge(ey_ready, T + tiles)

            step(0, 0, True, False)
            step(1, 1, True, True)
            with pe.Fori(1, ITS // 2) as i:
                step(2 * i, 0, True, True)
                step(2 * i + 1, 1, True, True)
            step(ITS, 0, False, True)

            for c in range(NT // 4):
                b, t0 = c // 2, 4 * (c % 2)
                pe.wait_ge(attn_ready, 2 * ITS)
                if c >= 2:
                    pe.wait_ge(yT_ready, c - 1)
                    pe.wait_ge(y_added, c - 1)
                for t in range(4):
                    last = pe.transpose(ps_a[c % 2][:, t * P:(t + 1) * P], attn[:, b, t0 + t, :, :].rearrange("p g d -> p (g d)"), identf[:, :])
                last.then_inc(yT_done, 1)
                pe.wait_ge(yT_ready, c + 1)
                for t in range(4):
                    last = pe.matmul(ps_b[c % 2][:, t * P:(t + 1) * P], prob[:, 0, t, 0:P], wo[:, :],
                                     start=True, stop=True)
                last.then_inc(y_done, 1)


def kernel(**inputs):
    import numpy as _np
    import concourse.bacc as _bacc
    from concourse import mybir as _mybir
    from concourse.bass_utils import run_bass_kernel_spmd as _run

    a = {n: _np.asarray(v) for n, v in inputs.items()}
    E, F, D = a["L0_ffn_W1"].shape
    host = {
        "x": a["L0_attn_x"],
        "wqkv": _np.concatenate([a["L0_attn_W_Q"].T, a["L0_attn_W_K"].T, a["L0_attn_W_V"].T], axis=1),
        "wo": a["L0_attn_W_O"].T,
        "wg": a["L0_ffn_Wg"].T,
        "w1": a["L0_ffn_W1"].reshape(E * F, D).T,
        "w3": a["L0_ffn_W3"].reshape(E * F, D).T,
        "w2": a["L0_ffn_W2"].transpose(0, 2, 1),
    }
    nc = _bacc.Bacc("TRN2", target_bir_lowering=False, num_devices=1)
    arrays, args = {}, []
    for name, v in host.items():
        v = _np.ascontiguousarray(v)
        arrays[f"in_{name}_dram"] = v
        args.append(nc.dram_tensor(f"in_{name}_dram", v.shape, _mybir.dt.from_np(v.dtype), kind="ExternalInput").ap())
    args.append(nc.dram_tensor("out_0_dram", a["L0_attn_x"].shape, _mybir.dt.float32, kind="ExternalOutput").ap())
    layer_kernel(nc, *args)
    r = _run(nc, [arrays], core_ids=[0])
    return r.results[0]["out_0_dram"]
```

```python
from contextlib import ExitStack

import concourse.bass as bass
from concourse import mybir

ALU = mybir.AluOpType
ACT = mybir.ActivationFunctionType
AX_X = mybir.AxisListType.X
F32 = mybir.dt.float32
BF16 = mybir.dt.bfloat16
U32 = mybir.dt.uint32

P = 128
NEG = -3.0e38


def layer_kernel(nc, x_in, wqkv_in, wo_in, wg_in, w1_in, w3_in, w2_in, out):
    NB, S, D = x_in.shape
    NH = 16
    HD = D // NH
    E = wg_in.shape[1]
    FH = w1_in.shape[1] // E
    FC = -(-FH // P)
    TAIL = FH - (FC - 1) * P
    HP = FC * P
    NT = NB * S // P
    TB = S // P
    G = 4
    NG = NH // G
    ITS = NB * NG
    CH = 512
    SCALE = float(HD) ** -0.5
    TERMS = 6
    KR = TERMS * HD
    Q_ROWS = [(0, 1, 3), (3, 2, 2), (4, 1, 1)]
    K_ROWS = [(2, 1, 3), (0, 5, 2), (1, 1, 1)]

    RING = 2
    WIDE = 4
    A_RING = 3
    PSLOTS = 4
    LAG = 2
    A_UNITS = []
    for i in range(TB):
        for c in range(i * P // CH + 1):
            together = max(1, min(G // 2, CH // min((i + 1) * P - c * CH, CH)))
            if i >= G and (i + 1) * P - c * CH == P:
                together = G
            A_UNITS += [(i, range(j, j + together), c) for j in range(0, G, together)]
    NA = len(A_UNITS)
    B_STEPS = [(c, k) for c in range(S // CH) for k in range((c + 1) * CH // P)]
    NS = len(B_STEPS)
    NBU = NS * G
    DIAG = TB
    O_COPY, O_TURN = (1, G + 1), (G, 2 * G)
    A_SPAN, M_TURN = 8.9, 9
    HID_AT = 1
    PV_AT = ((3, 3), (1, 3))
    Y_TURN = (4, 6, 10)
    GATHERS = (0, 0, 2, 2, 3, 3, 2, 1, 1, 1, 1, 0)

    def a_cols(u):
        i, heads, c = A_UNITS[u]
        return min((i + 1) * P - c * CH, CH)

    def b_first(n):
        c, k = B_STEPS[n]
        return max(k * P - c * CH, 0)

    def spread(span):
        cost = [len(A_UNITS[u][1]) * a_cols(u) + 80 for u in range(NA)]
        slots, done = [[] for _ in range(NS)], 0
        for u in range(NA):
            slots[min(int(done * span / sum(cost)), NS - 1)].append(u)
            done += cost[u]
        return slots

    a_slots = spread(A_SPAN)
    A_ORDER = []
    for n in range(NS):
        A_ORDER += [("sums", 1 - O_TURN.index(n))] if n in O_TURN else []
        A_ORDER += [("scores", u) for u in a_slots[n]]
        A_ORDER += [("maxima", 0)] if n == M_TURN else []
    assert len(A_ORDER) % A_RING == 0

    PAIRS = NB * S * 2
    TILES = (PAIRS + E * (P - 1)) // P
    FIRST = TILES - 6 * (ITS - 2)
    WALL = 6 * HP
    PIECES = 6

    def first_tile(s):
        if isinstance(s, int) and s == 1:
            return 0, FIRST
        return FIRST + (s - 2) * 6, 6

    def tile_of(s, n):
        k = n // 2 - (NS // 2 - first_tile(s)[1])
        return k if k >= 0 else None

    with ExitStack() as ctx:
        def sb(name, shape, dt):
            return ctx.enter_context(nc.sbuf_tensor(name, shape, dt))

        def sem(name):
            return ctx.enter_context(nc.semaphore(name))

        q_dram = nc.dram_tensor("q_parts", [NB * NH, KR, S], BF16).ap()
        k_dram = nc.dram_tensor("k_parts", [NB * NH, KR, S], BF16).ap()
        xs_dram = nc.dram_tensor("x_sorted", [(TILES + 1) * P, 2 * D], BF16).ap()
        y_dram = nc.dram_tensor("y_sorted", [TILES * P, D], F32).ap()

        bank = [ctx.enter_context(nc.psum_tensor(f"bank{i}", [P, CH], F32)) for i in range(8)]
        ring_a = (bank[0], bank[1], bank[7])
        ps_h, ps_o = (bank[4], bank[5]), bank[6]
        ps_p, turn_bank, ps_r = (bank[2], bank[3], bank[6], bank[7]), (bank[0], bank[1], bank[4], bank[5]), bank[6]
        ps_l = bank[0]
        yT_bank, y_bank = (bank[4], bank[4], bank[4], bank[0]), (bank[5], bank[5], bank[5], bank[1])
        ps_x, ps_y = ps_h[1][:, HP:CH].bitcast(BF16), ps_h[0][:, HP:CH]

        x = sb("x", [P, NT, D], F32)
        xn = sb("xn", [P, NT, D], F32)
        xhl = sb("xhl", [P, NT, 2, D], BF16)
        stats = sb("stats", [P, NT, 6], F32)
        mv = sb("mv", [P, NT, 2], F32)
        veps = sb("veps", [P, NT], F32)
        sdev = sb("sdev", [P, NT], F32)
        rstd = sb("rstd", [P, NT], F32)
        identf = sb("identf", [P, P], F32)
        identb = sb("identb", [P, P], BF16)
        before = sb("before", [P, P], BF16)
        onesb = sb("onesb", [P, P], BF16)
        causal = sb("causal", [P, P], BF16)
        iota_e = sb("iota_e", [P, E], F32)
        iota_t = sb("iota_t", [P, TILES], F32)
        iota_s = sb("iota_s", [P, NT], F32)
        lower = sb("lower", [P, E, E], F32)
        zrow = sb("zrow", [P, 2 * D], BF16)
        wqkv = sb("wqkv", [P, 3 * D], F32)
        wo = sb("wo", [P, D], F32)
        wg = sb("wg", [P, E], F32)
        rest = sb("rest", [P, 2, CH], F32)
        vall = sb("vall", [P, ITS, TB, G * HD], F32)
        vw = sb("vw", [P, 2, TB, G, 32], F32)
        qa = sb("qa", [P, 2, 2, S], BF16)
        ka = sb("ka", [P, 2, G, S], BF16)
        qb = sb("qb", [P, 2, 2, S], BF16)
        kb = sb("kb", [P, 2, G, S], BF16)
        mpart = sb("mpart", [P, 2, TB, G, 2], F32)
        nmax = sb("nmax", [P, TB, G], F32)
        nmr = sb("nmr", [P, 2, TB, G], F32)
        mt = sb("mt", [P, TB, 2, 3, 2], BF16)
        mrow = sb("mrow", [3 * G, S], BF16)
        prob = sb("prob", [P, PSLOTS, G, CH], F32)
        flat = prob[:, :, :, :].rearrange("p a b c -> p (a b c)").bitcast(BF16)
        part = [[flat[:, (3 * w + i) * NB * S:(3 * w + i + 1) * NB * S] for i in range(3)] for w in range(2)]
        osb = sb("osb", [P, CH], F32)
        rden = sb("rden", [P, 4, G], F32)
        attn = sb("attn", [P, NB, TB, NG, G * HD], F32)
        xnT = attn[:, :, :, :, :].rearrange("p b t g d -> p (b t g d)")
        lg = sb("lg", [P, NT, E], F32)
        sc = sb("sc", [P, NT, E], F32)
        r1 = sb("r1", [P, NT], F32)
        r2 = sb("r2", [P, NT], F32)
        top = sb("top", [P, NT, 8], F32)
        topi = sb("topi", [P, NT, 8], U32)
        topf = sb("topf", [P, NT, 8], F32)
        gate = sb("gate", [P, 2, NT], F32)
        hot = sb("hot", [P, 2, NT, E], F32)
        both = sb("both", [P, NT, E], BF16)
        big = sb("big", [P, TILES, E], F32)
        ntile = sb("ntile", [P, E], F32)
        start = sb("start", [P, E], F32)
        posf = sb("posf", [P, 2, NT], F32)
        pos = sb("pos", [P, 2, NT], U32)
        tile_f = sb("tile_f", [P, TILES], F32)
        tile_e = sb("tile_e", [P, TILES], U32)
        wall = sb("wall", [P, E, WALL], BF16)
        wbuf = sb("wbuf", [P, 2, WALL], BF16)
        wst = wbuf[:, :, :].rearrange("p q w -> p (q w)").bitcast(F32).rearrange("p (n w) -> p n w", n=PIECES)
        ysb = sb("ysb", [P, 2, D], F32)
        xn_flat = xn[:, :, :].rearrange("p t d -> p (t d)")
        th, ha, hf = [xn_flat[:, i * HP:(i + 1) * HP] for i in range(3)]
        xn16 = xn_flat[:, 3 * HP:].bitcast(BF16)
        hh, hl = xn16[:, 0:HP], xn16[:, HP:2 * HP]
        xs, xsT = [xn16[:, 2 * HP + i * 4 * D:2 * HP + (i + 1) * 4 * D].rearrange("p (q d) -> p q d", q=2)
                   for i in range(2)]
        yT = [xn_flat[:, q * CH:(q + 1) * CH] for q in range(2)]
        yg = wall[:, :, :].rearrange("p e w -> p (e w)").bitcast(F32)[:, 0:2 * NT * D].rearrange(
            "p (k t d) -> p k t d", k=2, t=NT)

        x_in_sem = [sem(f"x_in{b}") for b in range(NB)]
        wqkv_in_sem = sem("wqkv_in")
        w_in = sem("w_in")
        pool_const = sem("pool_const")
        pool_passed = sem("pool_passed")
        op_zero = sem("op_zero")
        mrow_one = sem("mrow_one")
        kb_one = sem("kb_one")
        pad_zero = sem("pad_zero")
        dve = sem("dve_chain")
        veps_ready = sem("veps_ready")
        sdev_ready = sem("sdev_ready")
        xn_ready = sem("xn_ready")
        xhi_ready = sem("xhi_ready")
        xlo_ready = sem("xlo_ready")
        xT_done = sem("xT_done")
        xnT_ready = sem("xnT_ready")
        qk_proj = sem("qk_proj")
        hi_ready = sem("hi_ready")
        rest_ready = sem("rest_ready")
        mid_ready = sem("mid_ready")
        lo_ready = sem("lo_ready")
        parts_out = sem("parts_out")
        v_proj = sem("v_proj")
        v_ready = sem("v_ready")
        logits_done = sem("logits_done")
        ex_in = sem("ex_in")
        ex_ready = sem("ex_ready")
        both_ready = sem("both_ready")
        rank_done = sem("rank_done")
        rank_read = sem("rank_read")
        pos_ready = sem("pos_ready")
        tile_e_ready = sem("tile_e_ready")
        xs_zero = sem("xs_zero")
        scattered = sem("scattered")
        a_loaded = [sem(f"a_loaded{i}") for i in range(2)]
        b_loaded = [sem(f"b_loaded{i}") for i in range(2)]
        m_loaded = sem("m_loaded")
        a_scores = sem("a_scores")
        a_used = sem("a_used")
        max_chain = sem("max_chain")
        mt_ready = sem("mt_ready")
        mT_done = sem("mT_done")
        mrow_ready = sem("mrow_ready")
        b_scores = sem("b_scores")
        exp_done = sem("exp_done")
        masked = sem("masked")
        vw_ready = sem("vw_ready")
        pv_done = sem("pv_done")
        osb_ready = sem("osb_ready")
        oT_done = sem("oT_done")
        rden_ready = sem("rden_ready")
        attn_ready = sem("attn_ready")
        yT_done = sem("yT_done")
        yT_ready = sem("yT_ready")
        y_done = sem("y_done")
        y_added = sem("y_added")
        w_stage = [sem(f"w_stage{i}") for i in range(PIECES)]
        w_hi = sem("w_hi")
        w_lo = sem("w_lo")
        w_tail = sem("w_tail")
        w13_here = [sem(f"w13_here{i}") for i in range(2)]
        w2_here = [sem(f"w2_here{i}") for i in range(2)]
        x_here = [sem(f"x_here{i}") for i in range(2)]
        xsT_done = sem("xsT_done")
        xsT_ready = sem("xsT_ready")
        h_done = sem("h_done")
        th_ready = sem("th_ready")
        ha_ready = sem("ha_ready")
        hf_ready = sem("hf_ready")
        hh_ready = sem("hh_ready")
        hl_ready = sem("hl_ready")
        ey_done = sem("ey_done")
        ey_ready = sem("ey_ready")
        ey_out = [sem(f"ey_out{i}") for i in range(2)]
        gathered = [sem(f"gathered{c}") for c in range(NT // 4)]
        combined = sem("combined")
        out_done = sem("out_done")

        nc.disable_value_cache = True
        block = ctx.enter_context(nc.Block())

        W_PIECES = [(k, e) for e in range(E) for k in range(3)]
        NW = len(W_PIECES)

        def w_areas(k):
            if k < 2:
                return [(slice(0, P), slice(0, FH))]
            return [(slice(0, P), slice(0, (FC - 1) * P)), (slice(0, TAIL), slice((FC - 1) * P, HP))]

        def w_part(buf, k, i, cols):
            return buf[:, (2 * k + i) * HP + cols.start:(2 * k + i) * HP + cols.stop]

        def has_down(s, n):
            if known(s, ITS):
                return n == 1
            k = tile_of(s, n)
            return n % 2 == 1 and k is not None and not (known(s, 1) and k == 0)

        def known(s, *values):
            return isinstance(s, int) and s in values

        def loads(s, par):
            return 16 * (s // 2 + 1) if isinstance(s, int) else 8 * (s - par) + 16

        def parity(s, k):
            return k % 2 if known(s, 1) else (k + FIRST) % 2

        def tile_loads(X, q):
            return 8 * (X - q) + 16

        def a_bank(s, what):
            return bank[7] if known(s, ITS) else ring_a[A_ORDER.index(what) % A_RING]

        def b_bank(s, u):
            return bank[(u + 2) % WIDE] if known(s, ITS - 1) else bank[2 + u % RING]

        def load_piece(eng, n):
            k, e = W_PIECES[n]
            slot = n % PIECES
            if n >= PIECES:
                eng.wait_ge(w_lo, n - PIECES + 1)
            if k < 2:
                eng.dma_start(wst[:, slot, 0:FH],
                              (w1_in, w3_in)[k][:, e * FH:(e + 1) * FH]).then_inc(w_stage[slot], 32)
            else:
                w = wst[:, slot, :].rearrange("p (c d) -> p c d", c=FC)
                eng.dma_start(w[:, 0:FC - 1, :],
                              w2_in[e, 0:(FC - 1) * P, :].rearrange("(c p) d -> p c d", p=P)).then_inc(w_stage[slot], 16)
                eng.dma_start(w[0:TAIL, FC - 1, :], w2_in[e, (FC - 1) * P:FH, :]).then_inc(w_stage[slot], 16)

        @block.sync
        def _(sp):
            for b in range(NB):
                sp.dma_start(x[:, b * TB:(b + 1) * TB, :],
                             x_in[b].rearrange("(t p) d -> p t d", p=P)).then_inc(x_in_sem[b], 16)
                if b == 0:
                    sp.dma_start(wqkv[:, :], wqkv_in).then_inc(wqkv_in_sem, 16)
            sp.dma_start(wo[:, :], wo_in).then_inc(w_in, 16)
            sp.dma_start(wg[:, :], wg_in).then_inc(w_in, 16)

            def parts(b, heads=slice(0, NH)):
                for w, (dram, rows) in enumerate(((q_dram, Q_ROWS), (k_dram, K_ROWS))):
                    for i, (first, every, times) in enumerate(rows):
                        here = slice(heads.start * HD, heads.stop * HD)
                        dst = dram.rearrange("h (d r) n -> (h d) r n", r=TERMS)[b * P:(b + 1) * P, :, :]
                        dst = dst[here, first:first + every * (times - 1) + 1:every, :]
                        src = part[w][i][here, b * S:(b + 1) * S].rearrange("p (o n) -> p o n", o=1)
                        sp.dma_start(dst, src.to_broadcast([here.stop - here.start, times, S])).then_inc(parts_out, 16)

            def load(s, dst_q, dst_k, par, done):
                for jj in range(2):
                    sp.dma_start(dst_q[64 * jj:64 * jj + KR, par, :, :],
                                 q_dram[bass.ds(s * G + jj, 2, step=2)].rearrange("a r n -> r a n")).then_inc(done, 16)
                    sp.dma_start(dst_k[64 * jj:64 * jj + KR, par, jj::2, :],
                                 k_dram[bass.ds(s * G + jj, 2, step=2)].rearrange("a r n -> r a n")).then_inc(done, 16)

            def load_a(s, par):
                load(s, qa, ka, par, a_loaded[par])

            def load_b(s, par):
                load(s, qb, kb, par, b_loaded[par])

            for n in range(PIECES):
                load_piece(sp, n)
            sp.wait_ge(pool_const, 15)
            sp.dma_start(xs_dram.rearrange("(p t) d -> p t d", t=TILES + 1),
                         zrow[:, :].rearrange("p (o d) -> p o d", o=1).to_broadcast([P, TILES + 1, 2 * D])).then_inc(xs_zero, 16)
            sp.wait_ge(lo_ready, 4)
            parts(0, slice(0, G))
            sp.wait_ge(op_zero, 2)
            sp.wait_ge(parts_out, 16 * 6)
            load_a(0, 0)
            parts(0, slice(G, NH))
            sp.wait_ge(op_zero, 8)
            sp.wait_ge(mrow_one, 1)
            for par in range(2):
                for jj in range(2):
                    r = 64 * jj + KR
                    sp.dma_start(kb[r:r + 3, par, jj::2, :], mrow[0:3, :].rearrange("p (h n) -> p h n", h=1).to_broadcast(
                        [3, 2, S])).then_inc(kb_one, 16)
            sp.wait_ge(lo_ready, 4 * NB)
            load_b(0, 0)
            parts(1)
            sp.wait_ge(parts_out, 16 * 6 * (NB + 1))

            def m_rows(s, par):
                sp.wait_ge(mrow_ready, s + 1)
                if not known(s, 0, 1):
                    sp.wait_ge(b_scores, NBU * (s - 1))
                for jj in range(2):
                    r = 64 * jj + KR
                    sp.dma_start(qb[r:r + 3, par, :, :], mrow[6 * jj:6 * jj + 6, :]).then_inc(m_loaded, 16)

            def load_x(X, q):
                sp.dma_start(xs[:, q, :], xs_dram[bass.ds(X * P, P), :]).then_inc(x_here[q], 16)

            def store_y(X, q):
                sp.wait_ge(ey_ready, X + 1)
                sp.dma_start(y_dram[bass.ds(X * P, P), :], ysb[:, q, :]).then_inc(ey_out[q], 16)

            def step(s, par):
                T, tiles = first_tile(s)
                if known(s, 1):
                    load(s, qa, ka, par, a_loaded[par])
                    load(s, qb, kb, par, b_loaded[par])
                    m_rows(0, 0)
                    sp.wait_ge(scattered, 16 * 2 * NT)
                    load_x(0, 0)
                    sp.wait_ge(w_lo, NW)
                    sp.wait_ge(tile_e_ready, 1)
                for k in range(tiles):
                    q = parity(s, k)
                    if not (known(s, 1) and k < 2):
                        sp.wait_ge(h_done, T + k - 1)
                    e = sp.value_load(tile_e[0:1, bass.ds(T + k, 1)], min_val=0, max_val=E - 1)
                    of_e = wall[:, bass.ds(e, 1), :].rearrange("p e w -> p (e w)")
                    sp.dma_start(wbuf[:, q, 0:4 * HP], of_e[:, 0:4 * HP]).then_inc(w13_here[q], 16)
                    if not (known(s, 1) and k == 0):
                        sp.wait_ge(xsT_done, T + k)
                    load_x(T + k + 1, 1 - q)
                    if not (known(s, 1) and k < 2):
                        sp.wait_ge(ey_done, T + k - 1)
                    sp.dma_start(wbuf[:, q, 4 * HP:WALL], of_e[:, 4 * HP:WALL]).then_inc(w2_here[q], 16)
                    if not (known(s, 1) and k < 2):
                        store_y(T + k - 2, q)
                    if k == 1 and not known(s, 1):
                        sp.wait_ge(b_scores, NBU * (s - 1))
                        load(s, qb, kb, par, b_loaded[par])
                    if k == tiles - 3 and not known(s, ITS - 1):
                        sp.wait_ge(a_scores, NA * s)
                        load(s + 1, qa, ka, 1 - par, a_loaded[1 - par])
                m_rows(s, par)

            step(1, 1)
            with sp.Fori(1, ITS // 2 - 1) as i:
                step(2 * i, 0)
                step(2 * i + 1, 1)
            step(ITS - 2, 0)
            step(ITS - 1, 1)
            for X in (TILES - 2, TILES - 1):
                store_y(X, X % 2)

            for c in range(NT // 4):
                b, t0 = c // 2, 4 * (c % 2)
                sp.wait_ge(combined, 8 * (c + 1))
                sp.dma_start(out[b].rearrange("(t p) d -> p t d", p=P)[:, t0:t0 + 4, :],
                             x[:, 4 * c:4 * c + 4, :]).then_inc(out_done, 16)
            sp.wait_ge(out_done, 16 * NT // 4)

        @block.gpsimd
        def _(pool):
            pool.memset(zrow[:, :], 0.0).then_inc(pool_const, 1)
            pool.memset(identf[:, :], 0.0).then_inc(pool_const, 1)
            pool.memset(identb[:, :], 0.0).then_inc(pool_const, 1)
            pool.memset(causal[:, :], 0.0).then_inc(pool_const, 1)
            pool.memset(before[:, :], 1.0).then_inc(pool_const, 1)
            pool.memset(onesb[:, :], 1.0).then_inc(pool_const, 1)
            pool.memset(mrow[:, :], 1.0).then_inc(mrow_one, 1)
            pool.memset(lower[:, :, :], 1.0).then_inc(pool_const, 1)
            pool.wait_ge(pool_const, 7)
            pool.affine_select(out=identf[:, :], in_=identf[:, :], compare_op=ALU.not_equal, fill=1.0,
                               base=0, pattern=[[-1, P]], channel_multiplier=1).then_inc(pool_const, 1)
            pool.affine_select(out=identb[:, :], in_=identb[:, :], compare_op=ALU.not_equal, fill=1.0,
                               base=0, pattern=[[-1, P]], channel_multiplier=1).then_inc(pool_const, 1)
            pool.affine_select(out=causal[:, :], in_=causal[:, :], compare_op=ALU.is_ge, fill=NEG,
                               base=0, pattern=[[-1, P]], channel_multiplier=1).then_inc(pool_const, 1)
            pool.affine_select(out=before[:, :], in_=before[:, :], compare_op=ALU.is_gt, fill=0.0,
                               base=0, pattern=[[1, P]], channel_multiplier=-1).then_inc(pool_const, 1)
            pool.affine_select(out=lower[:, :, :], in_=lower[:, :, :], compare_op=ALU.is_gt, fill=0.0,
                               base=0, pattern=[[1, E], [-1, E]], channel_multiplier=0).then_inc(pool_const, 1)
            pool.iota(iota_e[:, :], pattern=[[1, E]], base=0, channel_multiplier=0,
                      allow_small_or_imprecise_dtypes=True).then_inc(pool_const, 1)
            pool.iota(iota_t[:, :], pattern=[[1, TILES]], base=0, channel_multiplier=0,
                      allow_small_or_imprecise_dtypes=True).then_inc(pool_const, 1)
            pool.iota(iota_s[:, :], pattern=[[P, NT]], base=0, channel_multiplier=0,
                      allow_small_or_imprecise_dtypes=True).then_inc(pool_const, 1)
            for k in range(3):
                for i in range(2):
                    pad = slice(FH, HP) if k < 2 else slice((FC - 1) * P, HP)
                    pool.memset(wall[:, :, (2 * k + i) * HP + pad.start:(2 * k + i) * HP + pad.stop], 0.0).then_inc(pad_zero, 1)

            def zero(t, par):
                half = t[:, par, :, :].rearrange("p h n -> p (h n)").bitcast(F32)
                pool.memset(half, 0.0).then_inc(op_zero, 1)

            def zero_vw():
                pool.memset(vw[:, :, :, :, :], 0.0).then_inc(pool_const, 1)

            def one_vw():
                pool.wait_ge(pool_const, 17)
                pool.memset(vw[:, :, :, :, HD:HD + 1], 1.0).then_inc(pool_const, 1)

            operands = [(qa, 0), (ka, 0)]
            pool.memset(mpart[:, :, :, :, :], NEG).then_inc(pool_const, 1)

            pool.wait_ge(pad_zero, 6)
            for n, (k, e) in enumerate(W_PIECES):
                pool.wait_ge(w_hi, n + 1)
                areas = w_areas(k)
                for m, (rows, cols) in enumerate(areas):
                    if m:
                        pool.wait_ge(w_tail, n // 3 + 1)
                    last = pool.tensor_tensor(w_part(wall[rows, e, :], k, 1, cols), wst[rows, n % PIECES, cols],
                                              w_part(wall[rows, e, :], k, 0, cols), ALU.subtract)
                    if m < len(areas) - 1:
                        last.then_inc(w_tail, 1)
                last.then_inc(w_lo, 1)
                if n < len(operands):
                    zero(*operands[n])
                elif n == len(operands):
                    zero_vw()
                    one_vw()
                pool.wait_ge(w_lo, n + 1)
                if n >= NW - 2 * NT // 4 and n % 2:
                    c = (n - (NW - 2 * NT // 4)) // 2
                    pool.wait_ge(xhi_ready, c + 1)
                    pool.tensor_tensor(xhl[:, 4 * c:4 * c + 4, 1, :], xn[:, 4 * c:4 * c + 4, :],
                                       xhl[:, 4 * c:4 * c + 4, 0, :], ALU.subtract).then_inc(xlo_ready, 1)
            pool.wait_ge(xlo_ready, NT // 4)
            pool.wait_ge(pos_ready, 1)
            pool.wait_ge(xs_zero, 16)

            def scatter(k, t):
                pool.indirect_dma_start(
                    out=xs_dram, out_offset=bass.IndirectOffsetOnAxis(ap=pos[:, k, t:t + 1], axis=0),
                    in_=xhl[:, t, :, :].rearrange("p a d -> p (a d)"), in_offset=None).then_inc(scattered, 16)

            def gather(k, t):
                pool.indirect_dma_start(
                    out=yg[:, k, t, :], out_offset=None, in_=y_dram,
                    in_offset=bass.IndirectOffsetOnAxis(ap=pos[:, k, t:t + 1], axis=0)).then_inc(gathered[t // 4], 16)

            to_scatter = [(k, t) for k in range(2) for t in range(NT)]
            to_gather = [(k, t) for t in range(NT) for k in range(2)]
            for _ in range(28):
                scatter(*to_scatter.pop(0))
            pool.wait_ge(v_ready, NT // 4)

            def v_step(s, par):
                pool.tensor_copy(vw[:, par, :, :, 0:HD],
                                 vall[:, bass.ds(s, 1), :, :].rearrange("p a k (j d) -> p (a k) j d", j=G)).then_inc(vw_ready, 1)

            def step(s, par):
                T = first_tile(s)[0]
                for n, (c, k) in enumerate(B_STEPS):
                    X = None if known(s, ITS) else tile_of(s, n)
                    if k * P >= c * CH:
                        pool.wait_ge(exp_done, NBU * (s - 1) + G * (n + 1))
                        pool.sem_inc(pool_passed, 1)
                        part_k = prob[:, n % PSLOTS, :, 0:P]
                        pool.affine_select(out=part_k, in_=part_k, compare_op=ALU.is_ge, fill=0.0, base=0,
                                           pattern=[[0, G], [1, P]], channel_multiplier=-1).then_inc(masked, 1)
                    if X is not None and n % 2:
                        pool.wait_ge(hh_ready, T + X + 1)
                        if not (known(s, 1) and X == 0):
                            pool.wait_ge(ey_done, T + X)
                        pool.tensor_tensor(hl, hf, hh, ALU.subtract).then_inc(hl_ready, 1)
                    if n == G - 1 and not known(s, ITS):
                        if not known(s, 1):
                            pool.wait_ge(pv_done, NS * (s - 1))
                        v_step(s, par)
                    if known(s, 1):
                        for _ in range(min(2, len(to_scatter))):
                            scatter(*to_scatter.pop(0))
                    if known(s, ITS):
                        if n == 2:
                            for q in range(2):
                                pool.wait_ge(ey_out[q], 16 * ((TILES + 1 - q) // 2))
                        for _ in range(GATHERS[n]):
                            gather(*to_gather.pop(0))

            v_step(0, 0)
            step(1, 1)
            with pool.Fori(1, ITS // 2) as i:
                step(2 * i, 0)
                step(2 * i + 1, 1)
            step(ITS, 0)
            while to_gather:
                gather(*to_gather.pop(0))

        @block.scalar
        def _(act):
            pieces = iter(range(NW))

            def piece():
                n = next(pieces, None)
                if n is None:
                    return
                if n >= 3 and n + 3 < NW:
                    load_piece(act, n + 3)
                k, e = W_PIECES[n]
                if n == 0:
                    act.wait_ge(pad_zero, 6)
                act.wait_ge(w_stage[n % PIECES], 32 * (n // PIECES + 1))
                for rows, cols in w_areas(k):
                    last = act.activation(w_part(wall[rows, e, :], k, 0, cols), wst[rows, n % PIECES, cols], ACT.Copy)
                last.then_inc(w_hi, 1)

            zeros = zrow[:, :].bitcast(F32).rearrange("p (o d) -> p o d", o=1)

            def zero(t, par):
                half = t[:, par, :, :].rearrange("p h n -> p (h n)").bitcast(F32).rearrange("p (o d) -> p o d", d=D)
                act.activation(half, zeros.to_broadcast([P, half.shape[1], D]), ACT.Copy).then_inc(op_zero, 1)

            act.wait_ge(pool_const, 1)
            for t, par in ((qb, 0), (kb, 0), (qa, 1)):
                zero(t, par)
            for b in range(NB):
                if b == 1:
                    zero(ka, 1)
                act.wait_ge(veps_ready, b + 1)
                act.activation(sdev[:, b * TB:(b + 1) * TB], veps[:, b * TB:(b + 1) * TB], ACT.Sqrt).then_inc(sdev_ready, 1)

            def turned(c):
                act.wait_ge(xT_done, c + 1)
                act.activation(xnT[:, c * CH:(c + 1) * CH], turn_bank[c][:, :], ACT.Copy).then_inc(xnT_ready, 1)

            def hi(n):
                w, c = n % 2, n // 2
                act.wait_ge(qk_proj, n + 1)
                act.activation(part[w][0][:, c * CH:(c + 1) * CH], ps_p[n % 4][:, :], ACT.Copy).then_inc(hi_ready, 1)

            def mid(n):
                w, c = n % 2, n // 2
                act.wait_ge(rest_ready, n + 1)
                act.activation(part[w][1][:, c * CH:(c + 1) * CH], rest[:, n % 2, :], ACT.Copy).then_inc(mid_ready, 1)

            for _ in range(3):
                piece()
            turned(0)
            for c in range(NT // 4):
                if c < NT // 4 - 1:
                    turned(c + 1)
                hi(2 * c)
                if c:
                    mid(2 * c - 1)
                hi(2 * c + 1)
                mid(2 * c)
                for _ in range(2):
                    piece()
            mid(2 * (NT // 4) - 1)
            piece()
            act.wait_ge(ex_in, 1)
            act.activation(sc[:, :, :], lg[:, :, :], ACT.Exp).then_inc(ex_ready, 1)
            for c in range(NT // 4):
                act.activation(xhl[:, 4 * c:4 * c + 4, 0, :], xn[:, 4 * c:4 * c + 4, :], ACT.Copy).then_inc(xhi_ready, 1)
                piece()
            for _ in range(2):
                piece()
            for c in range(NT // 4):
                act.wait_ge(v_proj, c + 1)
                b, k0 = c // 2, 4 * (c % 2)
                for k in range(4):
                    last = act.activation(vall[:, b * NG:(b + 1) * NG, k0 + k, :],
                                          ps_h[c % 2][:, k * P:(k + 1) * P].rearrange("p (g d) -> p g d", g=NG), ACT.Copy)
                last.then_inc(v_ready, 1)
                piece()
            for t, par in ((qb, 1), (kb, 1)):
                zero(t, par)
                piece()
            for _ in range(NW):
                piece()
            act.wait_ge(parts_out, 16 * 6 * (NB + 1))

            def o_copy(s, c):
                act.wait_ge(pv_done, NS * s + (G if c == 0 else NS))
                if not (known(s, 0) and c == 0):
                    act.wait_ge(oT_done, 2 * s + c)
                act.activation(osb[:, :], ps_o[:, :], ACT.Copy).then_inc(osb_ready, 1)

            def m_copy(s, par):
                act.wait_ge(mT_done, s + 1)
                if not known(s, 0):
                    act.wait_ge(m_loaded, 32 * s)
                act.activation(mrow[:, :], a_bank(s, ("maxima", 0))[:, :].bitcast(BF16)[0:3 * G, :], ACT.Copy).then_inc(mrow_ready, 1)

            def y_turned(c):
                act.wait_ge(yT_done, c + 1)
                if c >= 2:
                    act.wait_ge(y_done, c - 1)
                act.activation(yT[c % 2], yT_bank[c][:, :], ACT.Copy).then_inc(yT_ready, 1)

            def x_copy(s, X, q):
                act.wait_ge(xsT_done, X + 1)
                if not (isinstance(X, int) and X < 2):
                    act.wait_ge(h_done, X - 1)
                act.activation(xsT[:, q, :], ps_x, ACT.Copy).then_inc(xsT_ready, 1)

            def step(s, par):
                T = first_tile(s)[0]
                for n in range(NS):
                    k = None if known(s, ITS) else tile_of(s, n)
                    N = CH - b_first(n)
                    for j in range(G):
                        u = n * G + j
                        act.wait_ge(b_scores, NBU * (s - 1) + u + 1)
                        if j == 0 and not (known(s, 1) and n < PSLOTS):
                            act.wait_ge(pv_done, NS * (s - 1) + n - PSLOTS + 1)
                        act.activation(prob[:, n % PSLOTS, j, 0:N], b_bank(s - 1, u)[:, 0:N],
                                       ACT.Exp, scale=SCALE).then_inc(exp_done, 1)
                    if n == O_COPY[0] and not known(s, 1):
                        o_copy(s - 2, 1)
                    if n == O_COPY[1]:
                        o_copy(s - 1, 0)
                    if known(s, ITS) and n - 1 in Y_TURN:
                        y_turned(Y_TURN.index(n - 1))
                    if known(s, 1) and n == NS - 2 * FIRST - 1:
                        x_copy(s, 0, 0)
                    if k is not None and n % 2 == 0:
                        act.wait_ge(h_done, T + k + 1)
                        if not (known(s, 1) and k == 0):
                            act.wait_ge(ha_ready, T + k)
                        act.activation(th, ps_h[0][:, 0:HP], ACT.Tanh, scale=0.5).then_inc(th_ready, 1)
                    if n == M_TURN and not known(s, ITS):
                        m_copy(s, par)
                    if has_down(s, n):
                        X, q = (TILES - 1, (TILES - 1) % 2) if known(s, ITS) else (T + k - 1, 1 - parity(s, k))
                        act.wait_ge(ey_done, X + 1)
                        if not (known(s, 1) and k < 3):
                            act.wait_ge(ey_out[q], tile_loads(X, q) - 16)
                        act.activation(ysb[:, q, :], ps_y, ACT.Copy).then_inc(ey_ready, 1)
                    if k is not None and n % 2:
                        x_copy(s, T + k + 1, 1 - parity(s, k))
                    if k is not None and n % 2:
                        act.wait_ge(hf_ready, T + k + 1)
                        act.activation(hh, hf, ACT.Copy).then_inc(hh_ready, 1)

            act.wait_ge(kb_one, 64)
            m_copy(0, 0)
            step(1, 1)
            with act.Fori(1, ITS // 2) as i:
                step(2 * i, 0)
                step(2 * i + 1, 1)
            step(ITS, 0)
            o_copy(ITS - 1, 1)
            y_turned(3)

        @block.vector
        def _(v):
            chain = [0]

            def link(ins):
                chain[0] += 1
                ins.then_inc(dve, 1)
                v.wait_ge(dve, chain[0])

            for b in range(NB):
                v.wait_ge(x_in_sem[b], 16)
                for t in range(b * TB, (b + 1) * TB):
                    last = v.bn_stats(stats[:, t, :], x[:, t, :])
                link(last)
                for t in range(b * TB, (b + 1) * TB):
                    last = v.bn_aggr(mv[:, t, :], stats[:, t, :])
                link(last)
                v.tensor_scalar(veps[:, b * TB:(b + 1) * TB], mv[:, b * TB:(b + 1) * TB, 1], 1e-5, None,
                                ALU.add).then_inc(veps_ready, 1)
            for b in range(NB):
                v.wait_ge(sdev_ready, b + 1)
                link(v.reciprocal(rstd[:, b * TB:(b + 1) * TB], sdev[:, b * TB:(b + 1) * TB]))
                for t in range(b * TB, (b + 1) * TB):
                    v.tensor_scalar(xn[:, t, :], x[:, t, :], mv[:, t, 0:1], rstd[:, t:t + 1],
                                    ALU.subtract, ALU.mult).then_inc(xn_ready, 1)
            for n in range(2 * NT // 4 + 1):
                if n < 2 * NT // 4:
                    w, c = n % 2, n // 2
                    v.wait_ge(hi_ready, n + 1)
                    if n >= 2:
                        v.wait_ge(lo_ready, n - 1)
                    v.tensor_tensor(rest[:, n % 2, :], ps_p[n % 4][:, :], part[w][0][:, c * CH:(c + 1) * CH],
                                    ALU.subtract).then_inc(rest_ready, 1)
                if n >= 1:
                    w, c = (n - 1) % 2, (n - 1) // 2
                    v.wait_ge(mid_ready, n)
                    v.tensor_tensor(part[w][2][:, c * CH:(c + 1) * CH], rest[:, (n - 1) % 2, :],
                                    part[w][1][:, c * CH:(c + 1) * CH], ALU.subtract).then_inc(lo_ready, 1)
            v.wait_ge(logits_done, 1)
            lps = ps_l[:, 0:NT * E].rearrange("p (t e) -> p t e", e=E)
            link(v.tensor_reduce(r1[:, :], lps, AX_X, ALU.max))

            def rows(a, n=E):
                return a.rearrange("p (t o) -> p t o", o=1).to_broadcast([P, a.shape[1], n])

            def cols(a, n):
                return a.rearrange("p (o e) -> p o e", o=1).to_broadcast([P, n, a.shape[1]])

            v.tensor_tensor(lg[:, :, :], lps, rows(r1[:, :]), ALU.subtract).then_inc(ex_in, 1)
            v.wait_ge(ex_ready, 1)
            link(v.tensor_reduce(r1[:, :], sc[:, :, :], AX_X, ALU.add))
            link(v.reciprocal(r2[:, :], r1[:, :]))
            link(v.tensor_tensor(lg[:, :, :], sc[:, :, :], rows(r2[:, :]), ALU.mult))
            for t in range(NT):
                last = v.max(top[:, t, :], lg[:, t, :])
            link(last)
            for t in range(NT):
                last = v.max_index(topi[:, t, :], top[:, t, :], lg[:, t, :])
            link(last)
            link(v.tensor_copy(topf[:, :, :], topi[:, :, :]))
            v.wait_ge(pool_const, 18)
            for k in range(2):
                last = v.tensor_tensor(hot[:, k, :, :], cols(iota_e[:, :], NT), rows(topf[:, :, k]), ALU.is_equal)
            link(last)
            v.tensor_tensor(both[:, :, :], hot[:, 0, :, :], hot[:, 1, :, :], ALU.add).then_inc(both_ready, 1)
            link(v.tensor_tensor(r1[:, :], top[:, :, 0], top[:, :, 1], ALU.add))
            link(v.tensor_scalar(r1[:, :], r1[:, :], 1e-20, None, ALU.add))
            link(v.reciprocal(r2[:, :], r1[:, :]))
            for k in range(2):
                last = v.tensor_tensor(gate[:, k, :], top[:, :, k], r2[:, :], ALU.mult)
            link(last)
            v.wait_ge(rank_done, 1)
            rank = ps_r[:, 0:NT * E].rearrange("p (t e) -> p t e", e=E)
            count = ps_r[:, NT * E:NT * E + E]
            big16 = big[:, 0:2 * E, :].rearrange("p a b -> p (a b)").rearrange("p (e s) -> p e s", e=E)
            link(v.tensor_tensor(big16, rows(count, NT), cols(iota_s[:, :], E), ALU.is_gt))
            link(v.tensor_reduce(ntile[:, :], big16, AX_X, ALU.add))
            link(v.tensor_tensor(big[:, 0:E, :], lower[:, :, :], cols(ntile[:, :], E), ALU.mult))
            link(v.tensor_reduce(start[:, :], big[:, 0:E, :], AX_X, ALU.add))
            link(v.tensor_tensor(big[:, :, :], cols(start[:, :], TILES), rows(iota_t[:, :]), ALU.is_le))
            link(v.tensor_reduce(tile_f[:, :], big[:, :, :], AX_X, ALU.add))
            v.tensor_scalar(tile_e[:, :], tile_f[:, :], -1.0, None, ALU.add).then_inc(tile_e_ready, 1)
            link(v.tensor_scalar(start[:, :], start[:, :], float(P), None, ALU.mult))
            v.tensor_tensor(lg[:, :, :], rank, cols(start[:, :], NT), ALU.add).then_inc(rank_read, 1)
            v.wait_ge(rank_read, 1)
            for k in range(2):
                link(v.tensor_tensor(sc[:, :, :], lg[:, :, :], hot[:, k, :, :], ALU.mult))
                link(v.tensor_reduce(posf[:, k, :], sc[:, :, :], AX_X, ALU.add))
            v.tensor_copy(pos[:, :, :], posf[:, :, :]).then_inc(pos_ready, 1)

            def row_max(s, par, u):
                i, heads, c = A_UNITS[u]
                N, H = a_cols(u), len(heads)
                v.wait_ge(a_scores, NA * s + u + 1)
                v.tensor_reduce(mpart[:, par, i, heads.start:heads.stop, c],
                                a_bank(s, ("scores", u))[:, 0:H * N].rearrange("p (h n) -> p h n", h=H),
                                AX_X, ALU.max).then_inc(a_used, 1)

            def by_jj(a):
                return a.rearrange("p t (h jj) -> p t h jj", jj=2)

            def mt_part(r):
                return mt[:, :, :, r, :].rearrange("p t jj h -> p t h jj")

            def split_max(s, par):
                v.wait_ge(a_used, NA * (s + 1))
                if not known(s, 0):
                    v.wait_ge(mT_done, s)
                v.tensor_reduce(nmax[:, :, :], mpart[:, par, :, :, :], AX_X, ALU.max, negate=True).then_inc(max_chain, 1)
                v.wait_ge(max_chain, 5 * s + 1)
                v.tensor_copy(mt_part(0), by_jj(nmax[:, :, :])).then_inc(max_chain, 1)
                v.wait_ge(max_chain, 5 * s + 2)
                v.tensor_tensor(by_jj(nmr[:, 0, :, :]), by_jj(nmax[:, :, :]), mt_part(0), ALU.subtract).then_inc(max_chain, 1)
                v.wait_ge(max_chain, 5 * s + 3)
                v.tensor_copy(mt_part(1), by_jj(nmr[:, 0, :, :])).then_inc(max_chain, 1)
                v.wait_ge(max_chain, 5 * s + 4)
                v.tensor_tensor(by_jj(nmr[:, 1, :, :]), by_jj(nmr[:, 0, :, :]), mt_part(1), ALU.subtract).then_inc(max_chain, 1)
                v.wait_ge(max_chain, 5 * s + 5)
                v.tensor_copy(mt_part(2), by_jj(nmr[:, 1, :, :])).then_inc(mt_ready, 1)

            def invert(s, c, o_bank):
                v.wait_ge(oT_done, 2 * s + c + 1)
                if not (known(s, 0) and c == 0):
                    v.wait_ge(attn_ready, 2 * s + c)
                o = o_bank[:, :].rearrange("p (t j d) -> p t j d", t=4, j=G)
                v.reciprocal(rden[:, :, :], o[:, :, :, HD]).then_inc(rden_ready, 1)

            def normalise(s, c, o_bank):
                v.wait_ge(rden_ready, 2 * s + c + 1)
                o = o_bank[:, :].rearrange("p (t j d) -> p t j d", t=4, j=G)
                dst = attn[:, bass.ds(s // NG, 1), 4 * c:4 * c + 4, bass.ds(s % NG, 1), :]
                v.tensor_tensor(dst.rearrange("p a t g (j d) -> p (a t g) j d", j=G), o[:, :, :, 0:HD],
                                rden[:, :, :].rearrange("p t (j o) -> p t j o", o=1).to_broadcast([P, 4, G, HD]),
                                ALU.mult).then_inc(attn_ready, 1)

            def add_attention(c):
                v.wait_ge(y_done, c + 1)
                v.tensor_tensor(x[:, 4 * c:4 * c + 4, :], y_bank[c][:, :].rearrange("p (t d) -> p t d", t=4),
                                x[:, 4 * c:4 * c + 4, :], ALU.add).then_inc(y_added, 1)

            def add_experts(c):
                v.wait_ge(y_added, c + 1)
                v.wait_ge(gathered[c], 16 * 8)
                for k in range(2):
                    if k:
                        v.wait_ge(combined, 8 * c + 4)
                    for t in range(4 * c, 4 * c + 4):
                        v.scalar_tensor_tensor(out=x[:, t, :], in0=yg[:, k, t, :], scalar=gate[:, k, t:t + 1],
                                               in1=x[:, t, :], op0=ALU.mult, op1=ALU.add).then_inc(combined, 1)

            def gate_1(s, k):
                T = first_tile(s)[0]
                v.wait_ge(th_ready, T + k + 1)
                if not (known(s, 1) and k == 0):
                    v.wait_ge(hf_ready, T + k)
                v.scalar_tensor_tensor(out=ha, in0=th, scalar=1.0, in1=ps_h[0][:, 0:HP],
                                       op0=ALU.add, op1=ALU.mult).then_inc(ha_ready, 1)

            def gate_3(s, k):
                T = first_tile(s)[0]
                v.wait_ge(ha_ready, T + k + 1)
                if not (known(s, 1) and k == 0):
                    v.wait_ge(hl_ready, T + k)
                v.scalar_tensor_tensor(out=hf, in0=ha, scalar=0.5, in1=ps_h[1][:, 0:HP],
                                       op0=ALU.mult, op1=ALU.mult).then_inc(hf_ready, 1)

            def step(s, par):
                for n in range(NS):
                    mine = [] if known(s, ITS) else list(a_slots[n])
                    other = n % 2 == 1 and not known(s, ITS) and tile_of(s, n) is not None
                    for place in range(max(4, len(mine))):
                        if place == 0 and other:
                            gate_1(s, tile_of(s, n))
                        if place < len(mine):
                            row_max(s, par, mine[place])
                        if place == 0 and other:
                            gate_3(s, tile_of(s, n))
                        for c, turned in ((1, s - 2), (0, s - 1)):
                            if n == O_TURN[1 - c] and not (known(s, 1) and c == 1):
                                if place == 0:
                                    invert(turned, c, a_bank(s, ("sums", c)))
                                if place == 1:
                                    normalise(turned, c, a_bank(s, ("sums", c)))
                    if NA - 1 in mine:
                        split_max(s, par)
                    if known(s, ITS) and n in (7, 9):
                        add_attention((n - 7) // 2)

            for u in range(NA):
                row_max(0, 0, u)
            split_max(0, 0)
            step(1, 1)
            with v.Fori(1, ITS // 2) as i:
                step(2 * i, 0)
                step(2 * i + 1, 1)
            step(ITS, 0)

            add_experts(0)
            add_attention(2)
            invert(ITS - 1, 1, bank[7])
            normalise(ITS - 1, 1, bank[7])
            add_attention(3)
            for c in range(1, NT // 4):
                add_experts(c)

        @block.tensor
        def _(pe):
            pe.wait_ge(pool_const, 15)
            for c in range(NT // 4 + 1):
                if c < NT // 4:
                    for t in range(4 * c, 4 * c + 4):
                        pe.wait_ge(xn_ready, t + 1)
                        last = pe.transpose(turn_bank[c][:, (t % 4) * P:(t % 4 + 1) * P], xn[:, t, :], identf[:, :])
                    last.then_inc(xT_done, 1)
                if c == 1:
                    pe.wait_ge(wqkv_in_sem, 16)
                if c >= 1:
                    pe.wait_ge(xnT_ready, c)
                    for n in (2 * c - 2, 2 * c - 1):
                        w = n % 2
                        if n >= 4:
                            pe.wait_ge(rest_ready, n - 3)
                        pe.matmul(ps_p[n % 4][:, :], wqkv[:, w * D:(w + 1) * D], xnT[:, (c - 1) * CH:c * CH],
                                  start=True, stop=True).then_inc(qk_proj, 1)
            pe.wait_ge(w_in, 32)
            for t in range(NT):
                last = pe.matmul(ps_l[:, t * E:(t + 1) * E], xnT[:, t * P:(t + 1) * P], wg[:, :], start=True, stop=True)
            last.then_inc(logits_done, 1)
            for t in range(NT):
                c = t // 4
                if c >= 2 and t % 4 == 0:
                    pe.wait_ge(v_ready, c - 1)
                last = pe.matmul(ps_h[c % 2][:, (t % 4) * P:(t % 4 + 1) * P], xnT[:, t * P:(t + 1) * P],
                                 wqkv[:, 2 * D:3 * D], start=True, stop=True)
                if t % 4 == 3:
                    last.then_inc(v_proj, 1)
            pe.wait_ge(both_ready, 1)
            pe.wait_ge(rest_ready, 2 * NT // 4)
            for t in range(NT):
                last = pe.matmul(ps_r[:, NT * E:NT * E + E], onesb[:, :], both[:, t, :], start=(t == 0), stop=(t == NT - 1))
            pe.matmul(ps_r[:, 0:E], before[:, :], both[:, 0, :], start=True, stop=True)
            pe.matmul(ps_r[:, E:NT * E], before[:, :], both[:, 1:NT, :].rearrange("p t e -> p (t e)"),
                      start=True, stop=False, skip_group_check=True)
            for t in reversed(range(NT - 1)):
                later = both[:, t, :].rearrange("p (o e) -> p o e", o=1).to_broadcast([P, NT - 1 - t, E])
                last = pe.matmul(ps_r[:, (t + 1) * E:NT * E], onesb[:, :], later, start=False, stop=(t == 0),
                                 skip_group_check=True)
            last.then_inc(rank_done, 1)
            pe.wait_ge(v_ready, NT // 4)
            pe.wait_ge(rest_ready, 2 * NT // 4)

            def bank_free(s, what):
                if known(s, ITS):
                    pe.wait_ge(a_used, NA * ITS)
                    pe.wait_ge(mrow_ready, ITS)
                    return
                place = A_ORDER.index(what) - A_RING
                while True:
                    if place < 0:
                        if known(s, 0):
                            return
                        s, place = s - 1, place + len(A_ORDER)
                    kind, index = A_ORDER[place]
                    if kind == "sums" and (known(s, 0) or known(s, 1) and index == 1):
                        place -= A_RING
                        continue
                    break
                if kind == "scores":
                    pe.wait_ge(a_used, NA * s + index + 1)
                elif kind == "sums":
                    pe.wait_ge(attn_ready, 2 * s - 1 - index)
                else:
                    pe.wait_ge(mrow_ready, s + 1)

            def a_unit(s, par, u):
                i, heads, c = A_UNITS[u]
                N, H = a_cols(u), len(heads)
                if u == 0:
                    pe.wait_ge(a_loaded[par], 4 * loads(s, par))
                bank_free(s, ("scores", u))
                to = a_bank(s, ("scores", u))[:, 0:H * N].rearrange("p (h n) -> p h n", h=H)
                diagonal = (i + 1) * P <= c * CH + CH
                for h, j in enumerate(heads):
                    last = pe.matmul(to[:, h, :], qa[:, par, j // 2, i * P:(i + 1) * P],
                                     ka[:, par, j, c * CH:c * CH + N], start=True, stop=not diagonal,
                                     skip_group_check=True)
                if diagonal:
                    mask = causal[:, :].rearrange("p (h n) -> p h n", h=1).to_broadcast([P, H, P])
                    last = pe.matmul(to[:, :, N - P:N], identb[:, :], mask, start=False, stop=True,
                                     skip_group_check=True)
                last.then_inc(a_scores, 1)

            def b_unit(s, par, u):
                n, j = u // G, u % G
                c, k = B_STEPS[n]
                q0 = b_first(n)
                if u == 0:
                    pe.wait_ge(b_loaded[par], 4 * loads(s, par))
                    pe.wait_ge(m_loaded, 32 * (s + 1))
                if known(s, ITS - 1) and u >= WIDE:
                    pe.wait_ge(exp_done, NBU * s + u + 1 - WIDE)
                elif not (known(s, 0) and u < RING) and not (known(s, ITS - 1) and u >= RING):
                    pe.wait_ge(exp_done, NBU * s + u + 1 - RING)
                pe.matmul(b_bank(s, u)[:, 0:CH - q0], kb[:, par, j, k * P:(k + 1) * P],
                          qb[:, par, j // 2, c * CH + q0:(c + 1) * CH], start=True, stop=True).then_inc(b_scores, 1)

            def pv(s, par, n, heads):
                c, k = B_STEPS[n]
                q0 = b_first(n)
                if heads[0] == 0:
                    if k * P >= c * CH:
                        pe.wait_ge(masked, DIAG * s + (k + 1))
                    else:
                        pe.wait_ge(exp_done, NBU * s + G * (n + 1))
                    if n == 0:
                        pe.wait_ge(vw_ready, s + 1)
                    if k == 0 and not (known(s, 0) and c == 0):
                        pe.wait_ge(osb_ready, 2 * s + c)
                for j in heads:
                    last = pe.matmul(ps_o[32 * j:32 * j + 32, q0:CH], vw[:, par, k, j, :],
                                     prob[:, n % PSLOTS, j, 0:CH - q0], start=(k == 0),
                                     stop=(k == (c + 1) * CH // P - 1), skip_group_check=True)
                if heads[-1] == G - 1:
                    last.then_inc(pv_done, 1)

            def o_turn(s, c, to):
                pe.wait_ge(osb_ready, 2 * s + c + 1)
                if isinstance(s, int) and s >= ITS - 2:
                    pe.wait_ge(attn_ready, 2 * s + c)
                for t in range(4):
                    last = pe.transpose(to[:, t * P:(t + 1) * P], osb[:, t * P:(t + 1) * P], identf[:, :])
                last.then_inc(oT_done, 1)

            def m_turn(s):
                pe.wait_ge(mt_ready, s + 1)
                bank_free(s, ("maxima", 0))
                to = a_bank(s, ("maxima", 0))[:, :].bitcast(BF16)
                for i in range(TB):
                    last = pe.transpose(to[0:3 * G, i * P:(i + 1) * P],
                                        mt[:, i, :, :, :].rearrange("p jj r h -> p (jj r h)"), identb[:, :])
                last.then_inc(mT_done, 1)

            PASSES = ((0, 0), (1, 0), (0, 1))

            def x_turn(s, X, q):
                if not (isinstance(X, int) and X == 0):
                    pe.wait_ge(hf_ready, X)
                pe.wait_ge(x_here[q], tile_loads(X, q))
                for i in range(2):
                    last = pe.transpose(ps_x[:, i * D:(i + 1) * D], xs[:, q, i * D:(i + 1) * D], identb[:, :])
                last.then_inc(xsT_done, 1)

            def hidden(s, k, f):
                T, q = first_tile(s)[0], parity(s, k)
                if f == 0:
                    pe.wait_ge(w13_here[q], tile_loads(T + k, q))
                    pe.wait_ge(xsT_ready, T + k + 1)
                    if not (known(s, 1) and k < 2):
                        pe.wait_ge(ey_ready, T + k - 1)
                cols = slice(f * P, (f + 1) * P)
                for w in range(2):
                    for i, (a, b) in enumerate(PASSES):
                        last = pe.matmul(ps_h[w][:, cols], w_part(wbuf[:, q, :], w, a, cols),
                                         xsT[:, q, b * D:(b + 1) * D], start=(i == 0), stop=(i == 2))
                if f == FC - 1:
                    last.then_inc(h_done, 1)

            def down(s, k):
                T, q = first_tile(s)[0], parity(s, k)
                pe.wait_ge(w2_here[q], tile_loads(T + k, q))
                pe.wait_ge(hl_ready, T + k + 1)
                if known(s, ITS):
                    pe.wait_ge(ey_ready, TILES - 1)
                else:
                    pe.wait_ge(ha_ready, T + k + 2)
                for i, (a, b) in enumerate(PASSES):
                    for f in range(FC):
                        cols = slice(f * P, (f + 1) * P)
                        last = pe.matmul(ps_y, (hh, hl)[b][:, cols], w_part(wbuf[:, q, :], 2, a, cols),
                                         start=(i == 0 and f == 0), stop=(i == 2 and f == FC - 1))
                last.then_inc(ey_done, 1)

            def y_turn(c):
                b, t0 = c // 2, 4 * (c % 2)
                pe.wait_ge(attn_ready, 2 * NG * (b + 1) - 1 + c % 2)
                if c == 0:
                    pe.wait_ge(ey_ready, TILES)
                else:
                    pe.wait_ge(yT_ready, c)
                for t in range(4):
                    last = pe.transpose(yT_bank[c][:, t * P:(t + 1) * P],
                                        attn[:, b, t0 + t, :, :].rearrange("p g d -> p (g d)"), identf[:, :])
                last.then_inc(yT_done, 1)

            def y_product(c):
                pe.wait_ge(yT_ready, c + 1)
                if c == 0:
                    pe.wait_ge(xsT_ready, TILES + 1)
                else:
                    pe.wait_ge(y_added, c)
                for t in range(4):
                    last = pe.matmul(y_bank[c][:, t * P:(t + 1) * P], yT[c % 2][:, t * P:(t + 1) * P], wo[:, :],
                                     start=True, stop=True)
                last.then_inc(y_done, 1)

            def step(s, par):
                for n in range(NS):
                    mine = [] if known(s, ITS) else list(a_slots[n])
                    k = None if known(s, ITS) else tile_of(s, n)
                    if n in O_TURN:
                        c = 1 - O_TURN.index(n)
                        mine = [("sums", c)] + mine if not (known(s, 1) and c) else mine
                    for j in range(G):
                        b_unit(s - 1, 1 - par, n * G + j)
                        for what in mine[j * len(mine) // G:(j + 1) * len(mine) // G]:
                            if isinstance(what, int):
                                a_unit(s, par, what)
                            else:
                                c = what[1]
                                bank_free(s, what)
                                o_turn(s - 1 - c, c, a_bank(s, what))
                        if k is not None and n % 2 == 0 and 0 <= j - HID_AT < FC:
                            hidden(s, k, j - HID_AT)
                        if j == G - 1 and n == M_TURN and not known(s, ITS):
                            m_turn(s)
                        for half, heads in enumerate(((0, 1), (2, 3))):
                            if j == PV_AT[n % 2][half]:
                                if n >= LAG:
                                    pv(s - 1, 1 - par, n - LAG, heads)
                                elif not known(s, 1):
                                    pv(s - 2, par, NS - LAG + n, heads)
                        if j == G - 1 and known(s, 1) and n == NS - 2 * FIRST - 1:
                            x_turn(s, 0, 0)
                    if has_down(s, n):
                        down(s, -1 if known(s, ITS) else k - 1)
                    if k is not None and n % 2:
                        x_turn(s, first_tile(s)[0] + k + 1, 1 - parity(s, k))
                    if known(s, ITS):
                        if n in (6, 8):
                            y_product((n - 6) // 2)
                        if n in Y_TURN:
                            y_turn(Y_TURN.index(n))

            for u in range(NA):
                a_unit(0, 0, u)
            m_turn(0)
            pe.wait_ge(rank_read, 1)
            pe.wait_ge(kb_one, 64)
            step(1, 1)
            with pe.Fori(1, ITS // 2) as i:
                step(2 * i, 0)
                step(2 * i + 1, 1)
            step(ITS, 0)
            for n in range(NS - LAG, NS):
                pv(ITS - 1, 1, n, range(G))
            o_turn(ITS - 1, 1, bank[7])

            y_product(2)
            y_turn(3)
            y_product(3)


def kernel(**inputs):
    import numpy as _np
    import concourse.bacc as _bacc
    from concourse import mybir as _mybir
    from concourse.bass_utils import run_bass_kernel_spmd as _run

    a = {n: _np.asarray(v) for n, v in inputs.items()}
    E, F, D = a["L0_ffn_W1"].shape
    host = {
        "x": a["L0_attn_x"],
        "wqkv": _np.concatenate([a["L0_attn_W_Q"].T, a["L0_attn_W_K"].T, a["L0_attn_W_V"].T], axis=1),
        "wo": a["L0_attn_W_O"].T,
        "wg": a["L0_ffn_Wg"].T,
        "w1": a["L0_ffn_W1"].reshape(E * F, D).T,
        "w3": a["L0_ffn_W3"].reshape(E * F, D).T,
        "w2": a["L0_ffn_W2"].transpose(0, 2, 1),
    }
    nc = _bacc.Bacc("TRN2", target_bir_lowering=False, num_devices=1)
    arrays, args = {}, []
    for name, v in host.items():
        v = _np.ascontiguousarray(v)
        arrays[f"in_{name}_dram"] = v
        args.append(nc.dram_tensor(f"in_{name}_dram", v.shape, _mybir.dt.from_np(v.dtype), kind="ExternalInput").ap())
    args.append(nc.dram_tensor("out_0_dram", a["L0_attn_x"].shape, _mybir.dt.float32, kind="ExternalOutput").ap())
    layer_kernel(nc, *args)
    r = _run(nc, [arrays], core_ids=[0])
    return r.results[0]["out_0_dram"]
```
